# Optimizing a Trainium2 kernel written in Bass

```python
import numpy as np
import jax
import jax.numpy as jnp

def _softmax(x, axis=-1):
    return jax.nn.softmax(x, axis=axis)

def _gelu(x):
    return jax.nn.gelu(x, approximate=True)

def _silu(x):
    return jax.nn.silu(x)

def _sigmoid(x):
    return jax.nn.sigmoid(x)

def _layernorm(x, axis=-1, eps=1e-05):
    m = jnp.mean(x, axis=axis, keepdims=True)
    v = jnp.var(x, axis=axis, keepdims=True)
    return (x - m) / jnp.sqrt(v + eps)

def _scatter_add(tgt, idx, src, axis=0):
    return tgt.at[idx].add(src)

def _segment_sum(src, seg, n):
    return jax.ops.segment_sum(src, seg, n)
kernel_name = 'mk_dlrm_tower_d1_rec_r8_4aaaaa'

def setup_inputs(seed: int=0):
    np.random.seed(seed)
    _w = jnp.asarray

    def _rec_inputs():
        import jax
        import jax.numpy as jnp
        _tk = jax.random.key(seed)
        dense_ctx = jax.random.normal(jax.random.fold_in(_tk, 190), (512, 16), jnp.float32)
        ids = jnp.stack([jax.random.randint(jax.random.fold_in(_tk, 200 + f), (512,), 0, v, jnp.int32) for f, v in enumerate([1000, 1250, 125000, 1000, 1000, 125000, 125000, 1250, 12500, 1250, 1000, 1000, 12500, 12500, 1000, 12500, 1250, 12500, 1000, 1000, 1000, 1250, 1250, 1250, 12500, 1000, 1250, 12500, 1250, 1000, 1000, 1250])], axis=1)
        tbl_0 = 0.05 * jax.random.normal(jax.random.fold_in(_tk, 500 + 0), (1000, 64), jnp.float32)
        tbl_1 = 0.05 * jax.random.normal(jax.random.fold_in(_tk, 500 + 1), (1250, 64), jnp.float32)
        tbl_2 = 0.05 * jax.random.normal(jax.random.fold_in(_tk, 500 + 2), (125000, 64), jnp.float32)
        tbl_3 = 0.05 * jax.random.normal(jax.random.fold_in(_tk, 500 + 3), (1000, 64), jnp.float32)
        tbl_4 = 0.05 * jax.random.normal(jax.random.fold_in(_tk, 500 + 4), (1000, 64), jnp.float32)
        tbl_5 = 0.05 * jax.random.normal(jax.random.fold_in(_tk, 500 + 5), (125000, 64), jnp.float32)
        tbl_6 = 0.05 * jax.random.normal(jax.random.fold_in(_tk, 500 + 6), (125000, 64), jnp.float32)
        tbl_7 = 0.05 * jax.random.normal(jax.random.fold_in(_tk, 500 + 7), (1250, 64), jnp.float32)
        tbl_8 = 0.05 * jax.random.normal(jax.random.fold_in(_tk, 500 + 8), (12500, 64), jnp.float32)
        tbl_9 = 0.05 * jax.random.normal(jax.random.fold_in(_tk, 500 + 9), (1250, 64), jnp.float32)
        tbl_10 = 0.05 * jax.random.normal(jax.random.fold_in(_tk, 500 + 10), (1000, 64), jnp.float32)
        tbl_11 = 0.05 * jax.random.normal(jax.random.fold_in(_tk, 500 + 11), (1000, 64), jnp.float32)
        tbl_12 = 0.05 * jax.random.normal(jax.random.fold_in(_tk, 500 + 12), (12500, 64), jnp.float32)
        tbl_13 = 0.05 * jax.random.normal(jax.random.fold_in(_tk, 500 + 13), (12500, 64), jnp.float32)
        tbl_14 = 0.05 * jax.random.normal(jax.random.fold_in(_tk, 500 + 14), (1000, 64), jnp.float32)
        tbl_15 = 0.05 * jax.random.normal(jax.random.fold_in(_tk, 500 + 15), (12500, 64), jnp.float32)
        tbl_16 = 0.05 * jax.random.normal(jax.random.fold_in(_tk, 500 + 16), (1250, 64), jnp.float32)
        tbl_17 = 0.05 * jax.random.normal(jax.random.fold_in(_tk, 500 + 17), (12500, 64), jnp.float32)
        tbl_18 = 0.05 * jax.random.normal(jax.random.fold_in(_tk, 500 + 18), (1000, 64), jnp.float32)
        tbl_19 = 0.05 * jax.random.normal(jax.random.fold_in(_tk, 500 + 19), (1000, 64), jnp.float32)
        tbl_20 = 0.05 * jax.random.normal(jax.random.fold_in(_tk, 500 + 20), (1000, 64), jnp.float32)
        tbl_21 = 0.05 * jax.random.normal(jax.random.fold_in(_tk, 500 + 21), (1250, 64), jnp.float32)
        tbl_22 = 0.05 * jax.random.normal(jax.random.fold_in(_tk, 500 + 22), (1250, 64), jnp.float32)
        tbl_23 = 0.05 * jax.random.normal(jax.random.fold_in(_tk, 500 + 23), (1250, 64), jnp.float32)
        tbl_24 = 0.05 * jax.random.normal(jax.random.fold_in(_tk, 500 + 24), (12500, 64), jnp.float32)
        tbl_25 = 0.05 * jax.random.normal(jax.random.fold_in(_tk, 500 + 25), (1000, 64), jnp.float32)
        tbl_26 = 0.05 * jax.random.normal(jax.random.fold_in(_tk, 500 + 26), (1250, 64), jnp.float32)
        tbl_27 = 0.05 * jax.random.normal(jax.random.fold_in(_tk, 500 + 27), (12500, 64), jnp.float32)
        tbl_28 = 0.05 * jax.random.normal(jax.random.fold_in(_tk, 500 + 28), (1250, 64), jnp.float32)
        tbl_29 = 0.05 * jax.random.normal(jax.random.fold_in(_tk, 500 + 29), (1000, 64), jnp.float32)
        tbl_30 = 0.05 * jax.random.normal(jax.random.fold_in(_tk, 500 + 30), (1000, 64), jnp.float32)
        tbl_31 = 0.05 * jax.random.normal(jax.random.fold_in(_tk, 500 + 31), (1250, 64), jnp.float32)
        _rk = jax.random.fold_in(_tk, 7)
        W_top1 = 0.0441942 * jax.random.normal(jax.random.fold_in(_tk, 801), (512, 512), jnp.float32)
        W_top2 = 0.0441942 * jax.random.normal(jax.random.fold_in(_tk, 802), (512, 256), jnp.float32)
        W_top3 = 0.0625 * jax.random.normal(jax.random.fold_in(_tk, 803), (256, 1), jnp.float32)
        b_top1 = jnp.zeros((512,), jnp.float32)
        b_top2 = jnp.zeros((256,), jnp.float32)
        return (dense_ctx, ids, tbl_0, tbl_1, tbl_2, tbl_3, tbl_4, tbl_5, tbl_6, tbl_7, tbl_8, tbl_9, tbl_10, tbl_11, tbl_12, tbl_13, tbl_14, tbl_15, tbl_16, tbl_17, tbl_18, tbl_19, tbl_20, tbl_21, tbl_22, tbl_23, tbl_24, tbl_25, tbl_26, tbl_27, tbl_28, tbl_29, tbl_30, tbl_31, W_top1, b_top1, W_top2, b_top2, W_top3)
    dense_ctx, ids, tbl_0, tbl_1, tbl_2, tbl_3, tbl_4, tbl_5, tbl_6, tbl_7, tbl_8, tbl_9, tbl_10, tbl_11, tbl_12, tbl_13, tbl_14, tbl_15, tbl_16, tbl_17, tbl_18, tbl_19, tbl_20, tbl_21, tbl_22, tbl_23, tbl_24, tbl_25, tbl_26, tbl_27, tbl_28, tbl_29, tbl_30, tbl_31, W_top1, b_top1, W_top2, b_top2, W_top3 = _rec_inputs()

    def _L0_rec_setup():
        import jax, jax.numpy as jnp
        import numpy as np
        B, F, E = (512, 32, 64)
        P = F * (F - 1) // 2
        key = jax.random.key(seed)
        k1, k2 = jax.random.split(key)
        x = jax.random.normal(k1, (B, F, E), dtype=jnp.float32)
        kernel = jax.random.normal(k2, (E, P, E), dtype=jnp.float32) * 0.05
        return {'x': x, 'kernel': kernel}
    _L0_rec_all = _L0_rec_setup()
    _L0_rec_in = {k: v for k, v in _L0_rec_all.items() if k in ('kernel',)}
    del _L0_rec_all
    return {'dense_ctx': dense_ctx, 'ids': ids, 'tbl_0': tbl_0, 'tbl_1': tbl_1, 'tbl_2': tbl_2, 'tbl_3': tbl_3, 'tbl_4': tbl_4, 'tbl_5': tbl_5, 'tbl_6': tbl_6, 'tbl_7': tbl_7, 'tbl_8': tbl_8, 'tbl_9': tbl_9, 'tbl_10': tbl_10, 'tbl_11': tbl_11, 'tbl_12': tbl_12, 'tbl_13': tbl_13, 'tbl_14': tbl_14, 'tbl_15': tbl_15, 'tbl_16': tbl_16, 'tbl_17': tbl_17, 'tbl_18': tbl_18, 'tbl_19': tbl_19, 'tbl_20': tbl_20, 'tbl_21': tbl_21, 'tbl_22': tbl_22, 'tbl_23': tbl_23, 'tbl_24': tbl_24, 'tbl_25': tbl_25, 'tbl_26': tbl_26, 'tbl_27': tbl_27, 'tbl_28': tbl_28, 'tbl_29': tbl_29, 'tbl_30': tbl_30, 'tbl_31': tbl_31, 'W_top1': W_top1, 'b_top1': b_top1, 'W_top2': W_top2, 'b_top2': b_top2, 'W_top3': W_top3, 'L0_rec_kernel': _L0_rec_in['kernel']}

def reference(dense_ctx, ids, tbl_0, tbl_1, tbl_2, tbl_3, tbl_4, tbl_5, tbl_6, tbl_7, tbl_8, tbl_9, tbl_10, tbl_11, tbl_12, tbl_13, tbl_14, tbl_15, tbl_16, tbl_17, tbl_18, tbl_19, tbl_20, tbl_21, tbl_22, tbl_23, tbl_24, tbl_25, tbl_26, tbl_27, tbl_28, tbl_29, tbl_30, tbl_31, W_top1, b_top1, W_top2, b_top2, W_top3, L0_rec_kernel):
    import jax
    import jax.numpy as jnp

    def _L0_rec_ref(x, kernel):
        import jax, jax.numpy as jnp
        import numpy as np
        B, F, E = (512, 32, 64)
        P = F * (F - 1) // 2
        nf = x.shape[1]
        row_idx, col_idx = np.triu_indices(nf, k=1)
        p = x[:, row_idx, :]
        q = x[:, col_idx, :]
        kp = jnp.einsum('bpe,fpe,bpf->bp', p, kernel, q)
        return kp
    e = jnp.stack([tbl_0[ids[:, 0]], tbl_1[ids[:, 1]], tbl_2[ids[:, 2]], tbl_3[ids[:, 3]], tbl_4[ids[:, 4]], tbl_5[ids[:, 5]], tbl_6[ids[:, 6]], tbl_7[ids[:, 7]], tbl_8[ids[:, 8]], tbl_9[ids[:, 9]], tbl_10[ids[:, 10]], tbl_11[ids[:, 11]], tbl_12[ids[:, 12]], tbl_13[ids[:, 13]], tbl_14[ids[:, 14]], tbl_15[ids[:, 15]], tbl_16[ids[:, 16]], tbl_17[ids[:, 17]], tbl_18[ids[:, 18]], tbl_19[ids[:, 19]], tbl_20[ids[:, 20]], tbl_21[ids[:, 21]], tbl_22[ids[:, 22]], tbl_23[ids[:, 23]], tbl_24[ids[:, 24]], tbl_25[ids[:, 25]], tbl_26[ids[:, 26]], tbl_27[ids[:, 27]], tbl_28[ids[:, 28]], tbl_29[ids[:, 29]], tbl_30[ids[:, 30]], tbl_31[ids[:, 31]]], axis=1)
    z = _L0_rec_ref(e, L0_rec_kernel)
    z = z.reshape(z.shape[0], -1)
    h = jnp.concatenate([z, dense_ctx], axis=1)
    h = jnp.maximum(h @ W_top1 + b_top1, 0.0)
    h = jnp.maximum(h @ W_top2 + b_top2, 0.0)
    y = h @ W_top3
    return y

_drawn_inputs = setup_inputs


def setup_inputs(seed=0):
    import zlib

    import numpy as np

    out = dict(_drawn_inputs(seed))
    spreads = {'b_top1': (0.0, 0.1), 'b_top2': (0.0, 0.1)}
    factors = {'tbl_0': 6.37,
     'tbl_1': 6.31,
     'tbl_2': 5.505,
     'tbl_3': 5.902,
     'tbl_4': 4.687,
     'tbl_5': 6.459,
     'tbl_6': 5.924,
     'tbl_7': 4.968,
     'tbl_8': 5.727,
     'tbl_9': 5.947,
     'tbl_10': 5.967,
     'tbl_11': 5.584,
     'tbl_12': 5.427,
     'tbl_13': 5.474,
     'tbl_14': 5.997,
     'tbl_15': 5.775,
     'tbl_16': 5.206,
     'tbl_17': 6.178,
     'tbl_18': 5.108,
     'tbl_19': 5.574,
     'tbl_20': 5.434,
     'tbl_21': 5.707,
     'tbl_22': 6.203,
     'tbl_23': 6.355,
     'tbl_24': 6.065,
     'tbl_25': 5.671,
     'tbl_26': 5.757,
     'tbl_27': 5.57,
     'tbl_28': 5.836,
     'tbl_29': 5.726,
     'tbl_30': 5.491,
     'tbl_31': 6.456}
    for name, (base, spread) in spreads.items():
        noise = np.random.default_rng([zlib.crc32(name.encode()), seed]).standard_normal(out[name].shape)
        drawn = base * np.exp(spread * noise) if base else spread * noise
        out[name] = jnp.asarray(drawn.astype(out[name].dtype))
    for name, factor in factors.items():
        out[name] = (out[name] * factor).astype(out[name].dtype)
    return out
```

```python
from contextlib import ExitStack

import concourse.bass as bass
import numpy as np
from concourse import mybir

F32 = mybir.dt.float32
F32R = mybir.dt.float32r
I32 = mybir.dt.int32
U32 = mybir.dt.uint32
ALU = mybir.AluOpType
ACT = mybir.ActivationFunctionType

P = 128
BATCH, FIELDS, EMB, DENSE = 512, 32, 64, 16
N1, N2 = 512, 256
BT = BATCH // P
BLOCKS = FIELDS // 2
TILES = [(i, m) for m in range(BLOCKS) for i in range(2 * m + 1)]
STEPS = len(TILES) // 2
GROUP = 64
GROUPS = len(TILES) // GROUP
CHUNK = 8
CHUNKS = len(TILES) // CHUNK
CW = CHUNK * P
CS = CHUNK // 2

NT = 3
NW = 8
NG = 4
NS = 2
NR = 3
NK = 5
W1_CHUNK = CHUNKS - NK
W1_AT = W1_CHUNK % NK
W1_STEPS = CS * (W1_CHUNK + 2)
assert W1_AT + 2 <= NK
Z_STEPS = TILES.index((2 * GROUPS - 1, BLOCKS - 1)) // 2 + 1

POOL_CHUNK = 24
POOL_STEP = 40
POOL_END = 118
POOL_EVERY = 4
SPLIT_AHEAD = 8
EARLY, LATE = 2, 7
TURN_AHEAD = (0, 2, 5)
LO_AHEAD = (0, 1, 4)
GATHER_AHEAD = 20
SUMS_STEPS, SUMS_LAG = 4, 2

H1_AT = GROUPS - 1
H2_AT = H1_AT + N1 // P
assert H2_AT + N2 // P < BLOCKS - 1

LO_AT = 32

SEL = 62
C_EYE, C_SEL, C_PLACE = 0, P, P + SEL
C_ALL = C_PLACE + GROUPS * P


def pair_index(a, b):
    i, j = FIELDS - 1 - b, FIELDS - 1 - a
    return i * (FIELDS - 1) - i * (i - 1) // 2 + (j - i - 1)


def z_row(tile, half):
    g, t = divmod(tile, GROUP)
    return g, 32 * (t % 4) + 2 * (t // 4) + half


def block_steps(m):
    return m * m // 2


def on_pool(s):
    return POOL_STEP <= s < POOL_END and (s - POOL_STEP) % POOL_EVERY == 0


def pool_steps(s):
    return sum(on_pool(x) for x in range(s))


def tower_kernel(nc, dense_t, ids, tables, w1, b1, w2, b2, w3, pairs, consts, out):
    turn_ahead = lambda m: TURN_AHEAD[(m >= EARLY) + (m >= LATE)]
    lo_ahead = lambda m: LO_AHEAD[(m >= EARLY) + (m >= LATE)]
    turn_at = {}
    x_lo_at = {}
    for m in range(BLOCKS):
        turn_at.setdefault(block_steps(m) - turn_ahead(m), []).append(m)
        x_lo_at.setdefault(block_steps(m) - lo_ahead(m), []).append(m)
    gather_at = {}
    for m in range(BLOCKS):
        for k in range(2 * BT):
            at = block_steps(m) - m + m * k // (2 * BT) - GATHER_AHEAD
            gather_at.setdefault(max(0, at), []).append((m, k))
    k_lo_at = {}
    k_hi_at = {}
    for c in range(CHUNKS):
        k_lo_at.setdefault(max(0, CS * (c - NK + 2)), []).append(c)
        k_hi_at.setdefault(max(0, CS * (c - NK + 2) - 2), []).append(c)

    with ExitStack() as ctx:

        def sb(name, shape, dt=F32):
            return ctx.enter_context(nc.sbuf_tensor(name, shape, dt))

        def psum(name, shape):
            return ctx.enter_context(nc.psum_tensor(name, shape, F32))

        def sem(name):
            return ctx.enter_context(nc.semaphore(name))

        cst = sb("cst", [P, C_ALL])
        eye = cst[:, C_EYE:C_EYE + P]
        ids_sb = sb("ids_sb", [P, BT, FIELDS], I32)
        dense_sb = sb("dense_sb", [DENSE, BATCH])
        dense_split = sb("dense_split", [P, BATCH], F32R)
        place = sb("place", [P, GROUPS * P], F32R)
        gathered = sb("gathered", [P, NG, BT, 2 * EMB])
        xt = sb("xt", [P, BLOCKS, BATCH])
        xs = sb("xs", [P, FIELDS - 1, BATCH], F32R)
        k_raw = sb("k_raw", [P, NR, CW])
        k_hi = sb("k_hi", [P, NK, CW], F32R)
        k_lo = sb("k_lo", [P, NK, CW], F32R)
        weighted = sb("weighted", [P, NW, 2, BATCH])
        staged = sb("staged", [P, NS, 2, BATCH])
        w1_sb = k_raw[:, 0:2, :].rearrange("p a (g n) -> p (a g) n", n=N1)
        w1_hi, w1_lo = (k[:, W1_AT:W1_AT + 2, :].rearrange("p a (g n) -> p (a g) n", n=N1) for k in (k_hi, k_lo))
        w2_sb = k_raw[:, 2, :].rearrange("p (g n) -> p g n", n=N2)
        w3_sb = sb("w3_sb", [P, N2 // P])
        b1_sb = sb("b1_sb", [P, N1 // P])
        b2_sb = sb("b2_sb", [P, N2 // P])
        h1 = xt[:, H1_AT:H1_AT + N1 // P, :]
        h2 = xt[:, H2_AT:H2_AT + N2 // P, :]
        y_sb = xt[0:1, H2_AT + N2 // P, :]
        z_kept = xt[:, 0:GROUPS - 1, :]
        z_hi = xs[:, 0:GROUPS, :]
        z_lo = xs[:, GROUPS:2 * GROUPS, :]

        product = psum("product", [P, NT, 2, BATCH])
        z_ps = psum("z_ps", [P, BATCH])
        turned = psum("turned", [P, BATCH])

        ids_in = sem("ids_in")
        cst_in = sem("cst_in")
        dense_in = sem("dense_in")
        weights_in = sem("weights_in")
        raw_in = [sem(f"raw_in{r}") for r in range(NR)]
        block_in = [sem(f"block_in{g}") for g in range(NG)]
        block_turned = sem("block_turned")
        block_hi = sem("block_hi")
        block_lo = sem("block_lo")
        chunk_hi = sem("chunk_hi")
        chunk_lo = sem("chunk_lo")
        chunk_lo_pool = sem("chunk_lo_pool")
        products_done = sem("products_done")
        staged_done = sem("staged_done")
        weighted_dve = sem("weighted_dve")
        weighted_pool = sem("weighted_pool")
        sums_done = sem("sums_done")
        dense_zero = sem("dense_zero")
        dense_hi = sem("dense_hi")
        dense_lo = sem("dense_lo")
        z_out = sem("z_out")
        z_hi_done = sem("z_hi_done")
        z_lo_done = sem("z_lo_done")
        w1_hi_done = sem("w1_hi_done")
        w1_lo_done = sem("w1_lo_done")
        h1_done = sem("h1_done")
        h1_ready = sem("h1_ready")
        h2_done = sem("h2_done")
        h2_ready = sem("h2_ready")
        y_done = sem("y_done")
        y_ready = sem("y_ready")
        y_out = sem("y_out")

        at = [(STEPS - 3) % NT, (STEPS - 2) % NT, (STEPS - 1) % NT]
        h1_ps = [turned[:, :], product[:, at[0], 0, :], product[:, at[0], 1, :], product[:, at[1], 0, :]]
        h2_ps = [product[:, at[2], 0, :], product[:, at[2], 1, :]]
        y_ps = z_ps[0:1, :]

        def wait_block_read(eng, m):
            eng.wait_ge(block_hi, m)
            eng.wait_ge(block_lo, m)

        def weighting_in1(s):
            m0, m1 = TILES[2 * s][1], TILES[2 * s + 1][1]
            if m0 == m1:
                return xt[:, m0:m0 + 1, :].to_broadcast([P, 2, BATCH])
            return xt[:, m0:m0 + 2, :]

        def wait_weighted(eng, steps):
            eng.wait_ge(weighted_dve, steps - pool_steps(steps))
            if pool_steps(steps):
                eng.wait_ge(weighted_pool, pool_steps(steps))

        def wait_product_free(eng, steps):
            eng.wait_ge(weighted_dve, steps - pool_steps(steps))
            if pool_steps(steps):
                eng.wait_ge(staged_done, pool_steps(steps))

        def wait_chunk_lo(eng, c):
            if c < POOL_CHUNK:
                eng.wait_ge(chunk_lo, c + 1)
            else:
                eng.wait_ge(chunk_lo_pool, c - POOL_CHUNK + 1)

        with nc.Block() as block:

            @block.sync
            def _(sp):
                sp.dma_start(ids_sb[:, :, :], ids.rearrange("(t p) f -> p t f", p=P)).then_inc(ids_in, 16)
                for c in range(CHUNKS):
                    if c >= NR:
                        wait_chunk_lo(sp, c - NR)
                    for half in range(2):
                        sp.dma_start(k_raw[64 * half:64 * half + 64, c % NR, :],
                                     pairs[:, c * CW:(c + 1) * CW]).then_inc(raw_in[c % NR], 16)
                    if c == 0:
                        sp.dma_start(cst[:, :], consts).then_inc(cst_in, 16)
                        sp.dma_start(dense_sb[:, :], dense_t).then_inc(dense_in, 16)
                wait_chunk_lo(sp, CHUNKS - 1)
                sp.dma_start(w1_sb, w1.rearrange("(g p) n -> p g n", p=P)).then_inc(weights_in, 16)
                sp.dma_start(w2_sb, w2.rearrange("(g p) n -> p g n", p=P)).then_inc(weights_in, 16)
                sp.dma_start(w3_sb[:, :], w3).then_inc(weights_in, 16)
                sp.dma_start(b1_sb[:, :], b1).then_inc(weights_in, 16)
                sp.dma_start(b2_sb[:, :], b2).then_inc(weights_in, 16)
                sp.wait_ge(y_ready, 1)
                sp.dma_start(out, y_sb).then_inc(y_out, 16)
                sp.wait_ge(y_out, 16)

            @block.gpsimd
            def _(pool):
                def gather(m, k):
                    if m >= NG and k == 0:
                        pool.wait_ge(block_turned, m - NG + 1)
                    half, t = divmod(k, BT)
                    field = FIELDS - 1 - (2 * m + half)
                    pool.indirect_dma_start(
                        gathered[:, m % NG, t, half * EMB:(half + 1) * EMB], None, tables[field],
                        bass.IndirectOffsetOnAxis(ap=ids_sb[:, t, field:field + 1].bitcast(U32), axis=0),
                    ).then_inc(block_in[m % NG], 16)

                def weighting(s):
                    pool.wait_ge(staged_done, pool_steps(s) + 1)
                    pool.wait_ge(sums_done, (s - NW) // 2 + 1)
                    pool.tensor_tensor(weighted[:, s % NW, :, :], staged[:, pool_steps(s) % NS, :, :],
                                       weighting_in1(s), ALU.mult).then_inc(weighted_pool, 1)

                pool.wait_ge(ids_in, 16)
                for s in range(STEPS):
                    for m, k in gather_at.get(s, ()):
                        gather(m, k)
                    for c in k_lo_at.get(s, ()):
                        if c >= POOL_CHUNK:
                            pool.wait_ge(chunk_hi, c + 1)
                            pool.tensor_tensor(k_lo[:, c % NK, :], k_raw[:, c % NR, :],
                                               k_hi[:, c % NK, :].bitcast(F32),
                                               ALU.subtract).then_inc(chunk_lo_pool, 1)
                    if on_pool(s):
                        weighting(s)
                pool.wait_ge(w1_hi_done, 1)
                pool.tensor_tensor(w1_lo, w1_sb, w1_hi.bitcast(F32), ALU.subtract).then_inc(w1_lo_done, 1)

            @block.tensor
            def _(pe):
                def turn_block(m):
                    pe.wait_ge(block_in[m % NG], 2 * BT * 16 * (m // NG + 1))
                    if m >= 1:
                        pe.wait_ge(block_hi, m)
                        pe.wait_ge(block_lo, m)
                    for t in range(BT):
                        mm = pe.transpose(turned[:, t * P:(t + 1) * P], gathered[:, m % NG, t, :], eye)
                    mm.then_inc(block_turned, 1)

                def products(s):
                    if s % CS == 0:
                        pe.wait_ge(chunk_hi, s // CS + 1)
                        wait_chunk_lo(pe, s // CS)
                    if s >= NT:
                        wait_product_free(pe, s - NT + 1)
                    for y in range(2):
                        t = 2 * s + y
                        i, m = TILES[t]
                        if i == 0:
                            pe.wait_ge(block_hi, m + 1)
                            pe.wait_ge(block_lo, m + 1)
                        col = slice((t % CHUNK) * P, (t % CHUNK + 1) * P)
                        slot = (t // CHUNK) % NK
                        pe.matmul(product[:, s % NT, y, :], k_hi[:, slot, col], xs[:, i, :],
                                  start=True, stop=False)
                        mm = pe.matmul(product[:, s % NT, y, :], k_lo[:, slot, col], xs[:, i, :],
                                       start=False, stop=True)
                    mm.then_inc(products_done, 1)

                def sums(q):
                    g, at = divmod(q, GROUP // 4)
                    if at == 0:
                        if g >= 1:
                            pe.wait_ge(z_out, g)
                        else:
                            pe.wait_ge(dense_lo, 1)
                        pe.matmul(z_ps[:, :], place[:, g * P:(g + 1) * P],
                                  dense_split[:, :], start=True, stop=False, skip_group_check=True)
                    wait_weighted(pe, 2 * q + 2)
                    for c in range(4):
                        mm = pe.matmul(z_ps[32 * c:32 * c + 32, :],
                                       cst[:, C_SEL + 30 - 2 * at:C_SEL + 62 - 2 * at],
                                       weighted[:, (2 * q + c // 2) % NW, c % 2, :],
                                       start=False, stop=(at == GROUP // 4 - 1), skip_group_check=True)
                    mm.then_inc(sums_done, 1)

                pe.wait_ge(cst_in, 16)
                for s in range(STEPS):
                    for m in turn_at.get(s, ()):
                        turn_block(m)
                    products(s)
                    done = s + 1 - SUMS_LAG
                    if done > 0 and done % SUMS_STEPS == 0:
                        for q in range((done - SUMS_STEPS) // 2, done // 2):
                            sums(q)

                def layer_1(n, groups):
                    rows = slice(n * P, (n + 1) * P)
                    for g in groups:
                        for w, z in ((w1_hi, z_hi), (w1_hi, z_lo), (w1_lo, z_hi)):
                            mm = pe.matmul(h1_ps[n], w[:, g, rows], z[:, g, :],
                                           start=(g == 0 and w is w1_hi and z is z_hi),
                                           stop=(g == GROUPS - 1 and w is w1_lo))
                    return mm

                pe.wait_ge(w1_hi_done, 1)
                pe.wait_ge(w1_lo_done, 1)
                pe.wait_ge(z_lo_done, 1)
                wait_block_read(pe, BLOCKS)
                layer_1(0, range(GROUPS - 1))
                wait_product_free(pe, STEPS - 2)
                layer_1(1, range(GROUPS - 1))
                layer_1(2, range(GROUPS - 1))
                wait_product_free(pe, STEPS - 1)
                layer_1(3, range(GROUPS - 1))
                for q in range((STEPS - SUMS_STEPS) // 2, STEPS // 2):
                    sums(q)
                pe.wait_ge(z_lo_done, 2)
                for n in range(N1 // P):
                    layer_1(n, [GROUPS - 1]).then_inc(h1_done, 1)

                wait_product_free(pe, STEPS)
                pe.wait_ge(weights_in, 5 * 16)
                for g in range(N1 // P):
                    pe.wait_ge(h1_ready, g + 1)
                    for n in range(N2 // P):
                        mm = pe.matmul(h2_ps[n], w2_sb[:, g, n * P:(n + 1) * P], h1[:, g, :],
                                       start=(g == 0), stop=(g == N1 // P - 1))
                        if g == N1 // P - 1:
                            mm.then_inc(h2_done, 1)
                for g in range(N2 // P):
                    pe.wait_ge(h2_ready, g + 1)
                    mm = pe.matmul(y_ps, w3_sb[:, g:g + 1], h2[:, g, :],
                                   start=(g == 0), stop=(g == N2 // P - 1))
                mm.then_inc(y_done, 1)

            @block.scalar
            def _(act):
                def block_hi_parts(m):
                    act.wait_ge(block_turned, m + 1)
                    act.activation(xs[0:64, 2 * m, :], turned[0:64, :], ACT.Copy)
                    if 2 * m + 1 < FIELDS - 1:
                        act.activation(xs[64:128, 2 * m + 1, :], turned[64:128, :], ACT.Copy)
                    act.activation(xt[:, m, :], turned[:, :], ACT.Copy).then_inc(block_hi, 1)

                def chunk_hi_part(c):
                    act.wait_ge(raw_in[c % NR], 32 * (c // NR + 1))
                    if c >= NK:
                        act.wait_ge(products_done, CS * (c - NK + 1))
                    act.activation(k_hi[:, c % NK, :], k_raw[:, c % NR, :], ACT.Copy).then_inc(chunk_hi, 1)

                def keep_z(g):
                    act.wait_ge(sums_done, (g + 1) * GROUP // 4)
                    act.activation(z_kept[:, g, :], z_ps[:, :], ACT.Copy).then_inc(z_out, 1)

                def stage(s):
                    act.wait_ge(products_done, s + 1)
                    n = pool_steps(s)
                    if n >= NS:
                        act.wait_ge(weighted_pool, n - NS + 1)
                    act.activation(staged[:, n % NS, :, :], product[:, s % NT, :, :],
                                   ACT.Copy).then_inc(staged_done, 1)

                act.wait_ge(dense_in, 16)
                act.wait_ge(cst_in, 16)
                act.wait_ge(dense_zero, 1)
                act.activation(dense_split[0:DENSE, :], dense_sb[:, :], ACT.Copy)
                act.activation(place[:, :], cst[:, C_PLACE:C_PLACE + GROUPS * P], ACT.Copy).then_inc(dense_hi, 1)
                for s in range(STEPS):
                    for c in k_hi_at.get(s, ()):
                        chunk_hi_part(c)
                    for m in turn_at.get(s, ()):
                        block_hi_parts(m)
                    if s % (GROUP // 2) == SUMS_LAG and s > SUMS_LAG:
                        keep_z(s // (GROUP // 2) - 1)
                    if on_pool(s):
                        stage(s)
                    if s == STEPS - SPLIT_AHEAD:
                        act.wait_ge(products_done, Z_STEPS)
                        act.activation(z_hi[:, 0:GROUPS - 1, :], z_kept, ACT.Copy).then_inc(z_hi_done, 1)
                        act.wait_ge(weights_in, 5 * 16)
                        act.wait_ge(products_done, W1_STEPS)
                        act.activation(w1_hi, w1_sb, ACT.Copy).then_inc(w1_hi_done, 1)
                act.wait_ge(sums_done, STEPS // 2)
                act.activation(z_hi[:, GROUPS - 1, :], z_ps[:, :], ACT.Copy).then_inc(z_hi_done, 1)
                for n in range(N1 // P):
                    act.wait_ge(h1_done, n + 1)
                    act.activation(h1[:, n, :], h1_ps[n], ACT.Relu,
                                   bias=b1_sb[:, n:n + 1]).then_inc(h1_ready, 1)
                for n in range(N2 // P):
                    act.wait_ge(h2_done, n + 1)
                    act.activation(h2[:, n, :], h2_ps[n], ACT.Relu,
                                   bias=b2_sb[:, n:n + 1]).then_inc(h2_ready, 1)
                act.wait_ge(y_done, 1)
                act.activation(y_sb, y_ps, ACT.Copy).then_inc(y_ready, 1)

            @block.vector
            def _(dve):
                def block_lo_parts(m):
                    dve.wait_ge(block_hi, m + 1)
                    op = dve.tensor_tensor(xs[64:128, 2 * m, :], turned[0:64, :],
                                           xs[0:64, 2 * m, :].bitcast(F32), ALU.subtract)
                    if 2 * m + 1 < FIELDS - 1:
                        op = dve.tensor_tensor(xs[0:64, 2 * m + 1, :], turned[64:128, :],
                                               xs[64:128, 2 * m + 1, :].bitcast(F32), ALU.subtract)
                    op.then_inc(block_lo, 1)

                def chunk_lo_part(c):
                    dve.wait_ge(chunk_hi, c + 1)
                    dve.tensor_tensor(k_lo[:, c % NK, :], k_raw[:, c % NR, :],
                                      k_hi[:, c % NK, :].bitcast(F32), ALU.subtract).then_inc(chunk_lo, 1)

                def weighting(s):
                    dve.wait_ge(products_done, s + 1)
                    if s >= NW:
                        dve.wait_ge(sums_done, (s - NW) // 2 + 1)
                    dve.tensor_tensor(weighted[:, s % NW, :, :], product[:, s % NT, :, :],
                                      weighting_in1(s), ALU.mult).then_inc(weighted_dve, 1)

                dve.memset(dense_split[:, :].bitcast(F32), 0.0).then_inc(dense_zero, 1)
                dve.wait_ge(dense_hi, 1)
                dve.tensor_tensor(dense_split[LO_AT:LO_AT + DENSE, :], dense_sb[:, :],
                                  dense_split[0:DENSE, :].bitcast(F32), ALU.subtract).then_inc(dense_lo, 1)
                for s in range(STEPS):
                    for c in k_lo_at.get(s, ()):
                        if c < POOL_CHUNK:
                            chunk_lo_part(c)
                    for m in x_lo_at.get(s, ()):
                        block_lo_parts(m)
                    if not on_pool(s):
                        weighting(s)
                    if s == STEPS - SPLIT_AHEAD + 2:
                        dve.wait_ge(z_hi_done, 1)
                        dve.tensor_tensor(z_lo[:, 0:GROUPS - 1, :], z_kept, z_hi[:, 0:GROUPS - 1, :].bitcast(F32),
                                          ALU.subtract).then_inc(z_lo_done, 1)
                dve.wait_ge(z_hi_done, 2)
                dve.tensor_tensor(z_lo[:, GROUPS - 1, :], z_ps[:, :], z_hi[:, GROUPS - 1, :].bitcast(F32),
                                  ALU.subtract).then_inc(z_lo_done, 1)


def _constants():
    c = np.zeros((P, C_ALL), np.float32)
    c[:, C_EYE:C_EYE + P] = np.eye(P, dtype=np.float32)
    c[0:64, C_SEL + 30] = 1
    c[64:128, C_SEL + 31] = 1
    for t, (i, m) in enumerate(TILES):
        if i == 2 * m:
            g, row = z_row(t, 0)
            c[[m, LO_AT + m], C_PLACE + g * P + row] = 1
    return c


def _layout(inputs):
    kernel_in = np.asarray(inputs["L0_rec_kernel"])
    w1_in = np.asarray(inputs["W_top1"])
    n_pairs = kernel_in.shape[1]
    pair_of = np.full(2 * len(TILES), -1)
    w1_row = np.zeros(GROUPS * P, int)
    for t, (i, m) in enumerate(TILES):
        for half in range(2):
            g, row = z_row(t, half)
            if 2 * m + half > i:
                pair_of[2 * t + half] = pair_index(i, 2 * m + half)
                w1_row[g * P + row] = pair_of[2 * t + half]
            else:
                w1_row[g * P + row] = n_pairs + m
    pairs = np.zeros((EMB, 2 * len(TILES), EMB), kernel_in.dtype)
    pairs[:, pair_of >= 0] = kernel_in[:, pair_of[pair_of >= 0]]
    arrays = {
        "dense_t": np.asarray(inputs["dense_ctx"]).T,
        "ids": np.asarray(inputs["ids"]),
        "w1": w1_in[w1_row],
        "b1": np.asarray(inputs["b_top1"]).reshape(N1 // P, P).T,
        "w2": np.asarray(inputs["W_top2"]),
        "b2": np.asarray(inputs["b_top2"]).reshape(N2 // P, P).T,
        "w3": np.asarray(inputs["W_top3"]).reshape(N2 // P, P).T,
        "pairs": pairs.reshape(EMB, -1),
        "consts": _constants(),
    }
    for f in range(FIELDS):
        arrays[f"tbl_{f}"] = np.asarray(inputs[f"tbl_{f}"])
    return {name: np.ascontiguousarray(a) for name, a in arrays.items()}


def kernel(**inputs):
    import concourse.bacc as bacc
    from concourse.bass_utils import run_bass_kernel_spmd

    nc = bacc.Bacc("TRN2", target_bir_lowering=False, num_devices=1)
    arrays = _layout(inputs)
    dram = {
        name: nc.dram_tensor(name, a.shape, mybir.dt.from_np(a.dtype), kind="ExternalInput").ap()
        for name, a in arrays.items()
    }
    out = nc.dram_tensor("out", (BATCH, 1), F32, kind="ExternalOutput").ap()
    tower_kernel(
        nc, dram["dense_t"], dram["ids"], [dram[f"tbl_{f}"] for f in range(FIELDS)], dram["w1"],
        dram["b1"], dram["w2"], dram["b2"], dram["w3"], dram["pairs"], dram["consts"],
        out.rearrange("b o -> o b"),
    )
    r = run_bass_kernel_spmd(nc, [arrays], core_ids=[0])
    return r.results[0]["out"]
```

```python
from contextlib import ExitStack

import concourse.bass as bass
import numpy as np
from concourse import mybir

F32 = mybir.dt.float32
F32R = mybir.dt.float32r
I32 = mybir.dt.int32
U32 = mybir.dt.uint32
ALU = mybir.AluOpType
ACT = mybir.ActivationFunctionType

P = 128
BATCH, FIELDS, EMB, DENSE = 512, 32, 64, 16
N1, N2 = 512, 256
BT = BATCH // P
BLOCKS = FIELDS // 2
TILES = [(i, m) for m in range(BLOCKS) for i in range(2 * m + 1)]
STEPS = len(TILES) // 2
GROUP = 64
GROUPS = len(TILES) // GROUP
CHUNK = 8
CHUNKS = len(TILES) // CHUNK
CW = CHUNK * P
CS = CHUNK // 2

LOOKED = 1
LOOKS = 2 * LOOKED
LOOK_ROWS = 125
LOOK_PASSES = 10
NO = 5

NT = 3
NW = 8
NG = 4
NS = 2
NR = 3
NK = 5
GUESTS = 3
GUEST_AT = FIELDS - 2 - 4 * GUESTS
USED_NUMBERS = 4 * GROUPS
USED_STEPS = TILES.index((USED_NUMBERS - 1, BLOCKS - 1)) // 2 + 1

POOL_CHUNK = 27
POOL_STEP = 28
POOL_END = 118
POOL_EVERY = 4
SPLIT_AHEAD = 6
TURN_AHEAD = (0, 0, 1, 1, 2, 1, 2, 3, 4, 7, 3, 5, 6, 5, 4, 3)
LO_AHEAD = (0, 0, 1, 1, 1, 1, 1, 2, 2, 4, 2, 4, 3, 4, 1, 2)
HI_AT = (0, 0, 2, 5, 6, 9, 9, 16)
LO_AT = (0, 1, 3, 4, 5, 8, 10, 12)
K_AFTER = 9
GATHER_AHEAD = 10
SUMS_STEPS, SUMS_LAG = 4, 2

H1_AT = GROUPS - 1
H2_AT = H1_AT + N1 // P
assert H2_AT + N2 // P < BLOCKS - 1

DENSE_LO_AT = 32

SEL = 62
FOLD = 64 + P
C_ROW = 0
C_FOLD = C_ROW + LOOKS * LOOK_PASSES
C_EYE = C_FOLD + FOLD
C_SEL = C_EYE + P
C_PLACE = C_SEL + SEL
C_ALL = C_PLACE + GROUPS * P
TABLE_ROWS = [1250, 1000, 1000, 1250]


def pair_index(a, b):
    i, j = FIELDS - 1 - b, FIELDS - 1 - a
    return i * (FIELDS - 1) - i * (i - 1) // 2 + (j - i - 1)


def z_row(tile, half):
    g, t = divmod(tile, GROUP)
    return g, 32 * (t % 4) + 2 * (t // 4) + half


def block_steps(m):
    return m * m // 2


def on_pool(s):
    return POOL_STEP <= s < POOL_END and (s - POOL_STEP) % POOL_EVERY == 0


def pool_steps(s):
    return sum(on_pool(x) for x in range(s))


def tower_kernel(nc, dense_t, ids, ids_t, tables, w1, b1, w2, b2, w3, pairs, consts, out):
    turn_at = {}
    x_lo_at = {}
    for m in range(BLOCKS):
        turn_at.setdefault(block_steps(m) - TURN_AHEAD[m], []).append(m)
        x_lo_at.setdefault(block_steps(m) - LO_AHEAD[m], []).append(m)
    gather_at = {}
    for m in range(LOOKED, BLOCKS):
        for k in range(2 * BT):
            at = block_steps(m) - m + m * k // (2 * BT) - GATHER_AHEAD
            gather_at.setdefault(max(0, at), []).append((m, k))
    k_lo_at = {}
    k_hi_at = {}
    for c in range(CHUNKS):
        k_hi_at.setdefault(HI_AT[c] if c < len(HI_AT) else CS * (c - NK) + K_AFTER - 2, []).append(c)
        k_lo_at.setdefault(LO_AT[c] if c < len(LO_AT) else CS * (c - NK) + K_AFTER, []).append(c)

    with ExitStack() as ctx:

        def sb(name, shape, dt=F32):
            return ctx.enter_context(nc.sbuf_tensor(name, shape, dt))

        def psum(name, shape):
            return ctx.enter_context(nc.psum_tensor(name, shape, F32))

        def sem(name):
            return ctx.enter_context(nc.semaphore(name))

        cst = sb("cst", [P, C_ALL])
        eye = cst[:, C_EYE:C_EYE + P]
        ids_sb = sb("ids_sb", [P, BT, FIELDS], I32)
        dense_sb = sb("dense_sb", [DENSE, BATCH])
        dense_split = sb("dense_split", [P, BATCH], F32R)
        place = sb("place", [P, GROUPS * P], F32R)
        gathered = sb("gathered", [P, NG, BT, 2 * EMB])
        xt = sb("xt", [P, BLOCKS, BATCH])
        xs = sb("xs", [P, FIELDS - 1, BATCH], F32R)
        guests = [
            [xs[:, n:n + 2, :].rearrange("p a b -> p (a b)") for n in (GUEST_AT + 4 * x, GUEST_AT + 4 * x + 2)]
            for x in reversed(range(GUESTS))
        ]
        passes = [rows // LOOK_ROWS for rows in TABLE_ROWS[:LOOKS]]
        table_raw = [
            xt[0:LOOK_ROWS, BLOCKS - 2 * (n + 1):BLOCKS - 2 * n, :].rearrange("p a b -> p (a b)")[:, 0:passes[n] * EMB]
            .rearrange("p (k e) -> p k e", e=EMB) for n in range(LOOKS)
        ]
        ids_row = [xt[0:LOOK_ROWS, BLOCKS - 2 * LOOKS - 1 - n, :].bitcast(I32) for n in range(LOOKS)]
        table_split = [
            xs[0:LOOK_ROWS, n:n + 3, :].rearrange("p a b -> p (a b)")[:, 0:passes[x] * 2 * EMB]
            .rearrange("p (k h e) -> p k h e", h=2, e=EMB) for x, n in enumerate([8, 11, 8, 11][:LOOKS])
        ]
        one_hot = [xs[0:LOOK_ROWS, n, :] for n in (14, 15, 16, 17, FIELDS - 2)]
        fold = sb("fold", [P, FOLD], F32R)
        k_raw = sb("k_raw", [P, NR, CW])
        k_hi = sb("k_hi", [P, NK, CW], F32R)
        k_lo = sb("k_lo", [P, NK, CW], F32R)
        weighted = sb("weighted", [P, NW, 2, BATCH])
        staged = sb("staged", [P, NS, 2, BATCH])
        w1_sb = k_raw[:, 0:2, :].rearrange("p a (g n) -> p (a g) n", n=N1)
        w2_sb = k_raw[:, 2, :].rearrange("p (g n) -> p g n", n=N2)
        w3_sb = sb("w3_sb", [P, N2 // P])
        b1_sb = sb("b1_sb", [P, N1 // P])
        b2_sb = sb("b2_sb", [P, N2 // P])
        h1 = xt[:, H1_AT:H1_AT + N1 // P, :]
        h2 = xt[:, H2_AT:H2_AT + N2 // P, :]
        y_sb = xt[:, H2_AT + N2 // P, 0:BT]
        z_kept = xt[:, 0:GROUPS - 1, :]
        z_hi, z_lo, w1_hi, w1_lo = (xs[:, x * GROUPS:(x + 1) * GROUPS, :] for x in range(4))

        product = psum("product", [P, NT, 2, BATCH])
        z_ps = psum("z_ps", [P, BATCH])
        turned = psum("turned", [P, BATCH])

        ids_in = sem("ids_in")
        cst_look_in = sem("cst_look_in")
        cst_in = sem("cst_in")
        look_in = [sem(f"look_in{n}") for n in range(LOOKS)]
        fold_ready = sem("fold_ready")
        look_hi = sem("look_hi")
        look_lo = sem("look_lo")
        one_hot_ready = sem("one_hot_ready")
        one_hot_used = sem("one_hot_used")
        look_copied = sem("look_copied")
        dense_in = sem("dense_in")
        weights_in = sem("weights_in")
        raw_in = [sem(f"raw_in{r}") for r in range(NR)]
        block_in = [sem(f"block_in{g}") for g in range(NG)]
        block_turned = sem("block_turned")
        block_hi = sem("block_hi")
        block_lo = sem("block_lo")
        chunk_hi = sem("chunk_hi")
        chunk_lo = sem("chunk_lo")
        chunk_lo_pool = sem("chunk_lo_pool")
        products_done = sem("products_done")
        staged_done = sem("staged_done")
        weighted_dve = sem("weighted_dve")
        weighted_pool = sem("weighted_pool")
        sums_done = sem("sums_done")
        dense_zero = sem("dense_zero")
        dense_hi = sem("dense_hi")
        dense_lo = sem("dense_lo")
        z_out = sem("z_out")
        z_hi_done = sem("z_hi_done")
        z_lo_done = sem("z_lo_done")
        w1_hi_done = sem("w1_hi_done")
        w1_lo_done = sem("w1_lo_done")
        h1_done = sem("h1_done")
        h1_ready = sem("h1_ready")
        h2_done = sem("h2_done")
        h2_ready = sem("h2_ready")
        y_done = sem("y_done")
        y_ready = sem("y_ready")
        y_out = sem("y_out")

        at = [(STEPS - 3) % NT, (STEPS - 2) % NT, (STEPS - 1) % NT]
        h1_ps = [turned[:, :], product[:, at[0], 0, :], product[:, at[0], 1, :], product[:, at[1], 0, :]]
        h2_ps = [product[:, at[2], 0, :], product[:, at[2], 1, :]]
        y_ps = z_ps[:, 0:BT]

        def k_hi_buf(c):
            return guests[c - NK][0] if NK <= c < NK + GUESTS else k_hi[:, (c - GUESTS * (c >= NK)) % NK, :]

        def k_lo_buf(c):
            return guests[c - NK][1] if NK <= c < NK + GUESTS else k_lo[:, (c - GUESTS * (c >= NK)) % NK, :]

        def chunk_before(c):
            return c - NK if c - NK >= NK + GUESTS else c - NK - GUESTS

        def wait_block_read(eng, m):
            if m:
                eng.wait_ge(block_hi, m)
            if m > LOOKED:
                eng.wait_ge(block_lo, m - LOOKED)

        def weighting_in1(s):
            m0, m1 = TILES[2 * s][1], TILES[2 * s + 1][1]
            if m0 == m1:
                return xt[:, m0:m0 + 1, :].to_broadcast([P, 2, BATCH])
            return xt[:, m0:m0 + 2, :]

        def wait_weighted(eng, steps):
            eng.wait_ge(weighted_dve, steps - pool_steps(steps))
            if pool_steps(steps):
                eng.wait_ge(weighted_pool, pool_steps(steps))

        def wait_product_free(eng, steps):
            eng.wait_ge(weighted_dve, steps - pool_steps(steps))
            if pool_steps(steps):
                eng.wait_ge(staged_done, pool_steps(steps))

        def wait_chunk_lo(eng, c):
            if c < POOL_CHUNK:
                eng.wait_ge(chunk_lo, c + 1)
            else:
                eng.wait_ge(chunk_lo_pool, c - POOL_CHUNK + 1)

        with nc.Block() as block:

            @block.sync
            def _(sp):
                sp.dma_start(ids_sb[:, :, :], ids.rearrange("(t p) f -> p t f", p=P)).then_inc(ids_in, 16)
                sp.dma_start(cst[:, 0:C_EYE], consts[:, 0:C_EYE]).then_inc(cst_look_in, 16)
                for n in range(LOOKS):
                    field = FIELDS - 1 - n
                    sp.dma_start(table_raw[n], tables[field].rearrange("(p k) e -> p k e", p=LOOK_ROWS))\
                        .then_inc(look_in[n], 16)
                    sp.dma_start(ids_row[n], ids_t[field:field + 1, :].to_broadcast([LOOK_ROWS, BATCH]))\
                        .then_inc(look_in[n], 16)
                for c in range(CHUNKS):
                    if c >= NR:
                        wait_chunk_lo(sp, c - NR)
                    for half in range(2):
                        sp.dma_start(k_raw[64 * half:64 * half + 64, c % NR, :],
                                     pairs[:, c * CW:(c + 1) * CW]).then_inc(raw_in[c % NR], 16)
                    if c == 0:
                        sp.dma_start(cst[:, C_EYE:], consts[:, C_EYE:]).then_inc(cst_in, 16)
                        sp.dma_start(dense_sb[:, :], dense_t).then_inc(dense_in, 16)
                wait_chunk_lo(sp, CHUNKS - 1)
                sp.dma_start(w1_sb, w1.rearrange("(g p) n -> p g n", p=P)).then_inc(weights_in, 16)
                sp.dma_start(w2_sb, w2.rearrange("(g p) n -> p g n", p=P)).then_inc(weights_in, 16)
                sp.dma_start(w3_sb[:, :], w3).then_inc(weights_in, 16)
                sp.dma_start(b1_sb[:, :], b1).then_inc(weights_in, 16)
                sp.dma_start(b2_sb[:, :], b2).then_inc(weights_in, 16)
                sp.wait_ge(y_ready, 1)
                sp.dma_start(out, y_sb).then_inc(y_out, 16)
                sp.wait_ge(y_out, 16)

            @block.gpsimd
            def _(pool):
                def gather(m, k):
                    slot = (m - LOOKED) % NG
                    if m - LOOKED >= NG and k == 0:
                        pool.wait_ge(block_turned, m - NG + 1)
                    half, t = divmod(k, BT)
                    field = FIELDS - 1 - (2 * m + half)
                    pool.indirect_dma_start(
                        gathered[:, slot, t, half * EMB:(half + 1) * EMB], None, tables[field],
                        bass.IndirectOffsetOnAxis(ap=ids_sb[:, t, field:field + 1].bitcast(U32), axis=0),
                    ).then_inc(block_in[slot], 16)

                def weighting(s):
                    pool.wait_ge(staged_done, pool_steps(s) + 1)
                    pool.wait_ge(sums_done, (s - NW) // 2 + 1)
                    pool.tensor_tensor(weighted[:, s % NW, :, :], staged[:, pool_steps(s) % NS, :, :],
                                       weighting_in1(s), ALU.mult).then_inc(weighted_pool, 1)

                pool.wait_ge(ids_in, 16)
                for s in range(STEPS):
                    for m, k in gather_at.get(s, ()):
                        gather(m, k)
                    for c in k_lo_at.get(s, ()):
                        if c >= POOL_CHUNK:
                            pool.wait_ge(chunk_hi, c + 1)
                            pool.tensor_tensor(k_lo_buf(c), k_raw[:, c % NR, :],
                                               k_hi_buf(c).bitcast(F32),
                                               ALU.subtract).then_inc(chunk_lo_pool, 1)
                    if on_pool(s):
                        weighting(s)
                pool.wait_ge(w1_hi_done, 1)
                pool.tensor_tensor(w1_lo, w1_sb, w1_hi.bitcast(F32), ALU.subtract).then_inc(w1_lo_done, 1)

            @block.tensor
            def _(pe):
                def look_up(n):
                    pe.wait_ge(look_hi, n + 1)
                    pe.wait_ge(look_lo, n + 1)
                    for k in range(passes[n]):
                        done = sum(passes[:n]) + k
                        pe.wait_ge(one_hot_ready, done + 1)
                        pe.matmul(product[:, n // 2, n % 2, :], table_split[n][:, k, :, :], one_hot[done % NO],
                                  start=(k == 0), stop=(k == passes[n] - 1)).then_inc(one_hot_used, 1)

                def fold_block(m):
                    wait_block_read(pe, m)
                    pe.wait_ge(fold_ready, 1)
                    pe.wait_ge(look_copied, 2 * m + 2)
                    pe.matmul(turned[:, :], fold[:, 64:64 + P], xs[:, 2 * m, :], start=True, stop=False)
                    pe.matmul(turned[:, :], fold[:, 0:P], xs[:, 2 * m + 1, :], start=False, stop=True)\
                        .then_inc(block_turned, 1)

                def turn_block(m):
                    slot = (m - LOOKED) % NG
                    pe.wait_ge(block_in[slot], 2 * BT * 16 * ((m - LOOKED) // NG + 1))
                    wait_block_read(pe, m)
                    for t in range(BT):
                        mm = pe.transpose(turned[:, t * P:(t + 1) * P], gathered[:, slot, t, :], eye)
                    mm.then_inc(block_turned, 1)

                def products(s):
                    if s % CS == 0:
                        pe.wait_ge(chunk_hi, s // CS + 1)
                        wait_chunk_lo(pe, s // CS)
                    if s >= NT:
                        wait_product_free(pe, s - NT + 1)
                    for y in range(2):
                        t = 2 * s + y
                        i, m = TILES[t]
                        if i == 0:
                            wait_block_read(pe, m + 1)
                        col = slice((t % CHUNK) * P, (t % CHUNK + 1) * P)
                        c = t // CHUNK
                        pe.matmul(product[:, s % NT, y, :], k_hi_buf(c)[:, col], xs[:, i, :],
                                  start=True, stop=False)
                        mm = pe.matmul(product[:, s % NT, y, :], k_lo_buf(c)[:, col], xs[:, i, :],
                                       start=False, stop=True)
                    mm.then_inc(products_done, 1)

                def sums(q):
                    g, at = divmod(q, GROUP // 4)
                    if at == 0:
                        if g >= 1:
                            pe.wait_ge(z_out, g)
                        else:
                            pe.wait_ge(dense_lo, 1)
                        pe.matmul(z_ps[:, :], place[:, g * P:(g + 1) * P],
                                  dense_split[:, :], start=True, stop=False, skip_group_check=True)
                    wait_weighted(pe, 2 * q + 2)
                    for c in range(4):
                        mm = pe.matmul(z_ps[32 * c:32 * c + 32, :],
                                       cst[:, C_SEL + 30 - 2 * at:C_SEL + 62 - 2 * at],
                                       weighted[:, (2 * q + c // 2) % NW, c % 2, :],
                                       start=False, stop=(at == GROUP // 4 - 1), skip_group_check=True)
                    mm.then_inc(sums_done, 1)

                for m in range(LOOKED):
                    look_up(2 * m)
                    look_up(2 * m + 1)
                    fold_block(m)
                pe.wait_ge(cst_in, 16)
                for s in range(STEPS):
                    for m in turn_at.get(s, ()):
                        if m >= LOOKED:
                            turn_block(m)
                    products(s)
                    done = s + 1 - SUMS_LAG
                    if done > 0 and done % SUMS_STEPS == 0:
                        for q in range((done - SUMS_STEPS) // 2, done // 2):
                            sums(q)

                def layer_1(n, g, passes_of_g):
                    for w, z in passes_of_g:
                        mm = pe.matmul(h1_ps[n], w[:, g, n * P:(n + 1) * P], z[:, g, :],
                                       start=(g == 0 and w is w1_hi and z is z_hi),
                                       stop=(g == GROUPS - 1 and z is z_lo))
                    return mm

                z_hi_passes, z_lo_passes = ((w1_hi, z_hi), (w1_lo, z_hi)), ((w1_hi, z_lo),)

                def layer_1_kept(n):
                    for g in range(GROUPS - 1):
                        layer_1(n, g, z_hi_passes + z_lo_passes)

                pe.wait_ge(w1_hi_done, 1)
                pe.wait_ge(w1_lo_done, 1)
                pe.wait_ge(z_lo_done, 1)
                wait_block_read(pe, BLOCKS)
                layer_1_kept(0)
                wait_product_free(pe, STEPS - 2)
                layer_1_kept(1)
                layer_1_kept(2)
                for q in range((STEPS - SUMS_STEPS) // 2, STEPS // 2):
                    sums(q)
                wait_product_free(pe, STEPS - 1)
                layer_1_kept(3)
                pe.wait_ge(z_hi_done, 2)
                for n in range(N1 // P):
                    layer_1(n, GROUPS - 1, z_hi_passes)
                pe.wait_ge(z_lo_done, 2)
                for n in range(N1 // P):
                    layer_1(n, GROUPS - 1, z_lo_passes).then_inc(h1_done, 1)

                wait_product_free(pe, STEPS)
                pe.wait_ge(weights_in, 5 * 16)
                for g in range(N1 // P):
                    pe.wait_ge(h1_ready, g + 1)
                    for n in range(N2 // P):
                        mm = pe.matmul(h2_ps[n], w2_sb[:, g, n * P:(n + 1) * P], h1[:, g, :],
                                       start=(g == 0), stop=(g == N1 // P - 1))
                        if g == N1 // P - 1:
                            mm.then_inc(h2_done, 1)
                for g in range(N2 // P):
                    pe.wait_ge(h2_ready, g + 1)
                    for t in range(BT):
                        mm = pe.matmul(y_ps[:, t:t + 1], h2[:, g, t::BT], w3_sb[:, g:g + 1],
                                       start=(g == 0 and t == 0), stop=(g == N2 // P - 1), skip_group_check=True)
                mm.then_inc(y_done, 1)

            @block.scalar
            def _(act):
                def look_hi_part(n):
                    act.wait_ge(look_in[n], 32)
                    if n >= 2:
                        act.wait_ge(one_hot_used, sum(passes[:n - 1]))
                    act.activation(table_split[n][:, :, 0, :], table_raw[n], ACT.Copy).then_inc(look_hi, 1)

                def looked_up_block(m):
                    for n in (2 * m, 2 * m + 1):
                        act.wait_ge(one_hot_used, sum(passes[:n + 1]))
                        act.activation(xs[:, n, :], product[:, n // 2, n % 2, :], ACT.Copy).then_inc(look_copied, 1)
                    act.wait_ge(block_turned, m + 1)
                    act.activation(xt[:, m, :], turned[:, :], ACT.Copy).then_inc(block_hi, 1)

                def block_hi_parts(m):
                    act.wait_ge(block_turned, m + 1)
                    if m == GUEST_AT // 2:
                        act.wait_ge(products_done, CS * (NK + GUESTS))
                    act.activation(xs[0:64, 2 * m, :], turned[0:64, :], ACT.Copy)
                    if 2 * m + 1 < FIELDS - 1:
                        act.activation(xs[64:128, 2 * m + 1, :], turned[64:128, :], ACT.Copy)
                    act.activation(xt[:, m, :], turned[:, :], ACT.Copy).then_inc(block_hi, 1)

                def chunk_hi_part(c):
                    act.wait_ge(raw_in[c % NR], 32 * (c // NR + 1))
                    if c >= NK + GUESTS:
                        act.wait_ge(products_done, CS * (chunk_before(c) + 1))
                    act.activation(k_hi_buf(c), k_raw[:, c % NR, :], ACT.Copy).then_inc(chunk_hi, 1)

                def keep_z(g):
                    act.wait_ge(sums_done, (g + 1) * GROUP // 4)
                    act.activation(z_kept[:, g, :], z_ps[:, :], ACT.Copy).then_inc(z_out, 1)

                def stage(s):
                    act.wait_ge(products_done, s + 1)
                    n = pool_steps(s)
                    if n >= NS:
                        act.wait_ge(weighted_pool, n - NS + 1)
                    act.activation(staged[:, n % NS, :, :], product[:, s % NT, :, :],
                                   ACT.Copy).then_inc(staged_done, 1)

                act.wait_ge(cst_look_in, 16)
                act.activation(fold[:, :], cst[:, C_FOLD:C_FOLD + FOLD], ACT.Copy).then_inc(fold_ready, 1)
                for n in range(LOOKS):
                    look_hi_part(n)
                act.wait_ge(dense_in, 16)
                act.wait_ge(cst_in, 16)
                act.wait_ge(dense_zero, 1)
                act.activation(dense_split[0:DENSE, :], dense_sb[:, :], ACT.Copy)
                act.activation(place[:, :], cst[:, C_PLACE:C_PLACE + GROUPS * P], ACT.Copy).then_inc(dense_hi, 1)
                for s in range(STEPS):
                    for c in k_hi_at.get(s, ()):
                        chunk_hi_part(c)
                    for m in turn_at.get(s, ()):
                        if m < LOOKED:
                            looked_up_block(m)
                        else:
                            block_hi_parts(m)
                    if s % (GROUP // 2) == SUMS_LAG and s > SUMS_LAG:
                        keep_z(s // (GROUP // 2) - 1)
                    if on_pool(s):
                        stage(s)
                    if s == STEPS - SPLIT_AHEAD:
                        act.wait_ge(products_done, USED_STEPS)
                        act.activation(z_hi[:, 0:GROUPS - 1, :], z_kept, ACT.Copy).then_inc(z_hi_done, 1)
                        act.wait_ge(weights_in, 5 * 16)
                        act.activation(w1_hi, w1_sb, ACT.Copy).then_inc(w1_hi_done, 1)
                act.wait_ge(sums_done, STEPS // 2)
                act.activation(z_hi[:, GROUPS - 1, :], z_ps[:, :], ACT.Copy).then_inc(z_hi_done, 1)
                for n in range(N1 // P):
                    act.wait_ge(h1_done, n + 1)
                    act.activation(h1[:, n, :], h1_ps[n], ACT.Relu,
                                   bias=b1_sb[:, n:n + 1]).then_inc(h1_ready, 1)
                for n in range(N2 // P):
                    act.wait_ge(h2_done, n + 1)
                    act.activation(h2[:, n, :], h2_ps[n], ACT.Relu,
                                   bias=b2_sb[:, n:n + 1]).then_inc(h2_ready, 1)
                act.wait_ge(y_done, 1)
                act.activation(y_sb, y_ps, ACT.Copy).then_inc(y_ready, 1)

            @block.vector
            def _(dve):
                def look(n):
                    dve.wait_ge(look_hi, n + 1)
                    dve.tensor_tensor(table_split[n][:, :, 1, :], table_raw[n],
                                      table_split[n][:, :, 0, :].bitcast(F32), ALU.subtract).then_inc(look_lo, 1)
                    for k in range(passes[n]):
                        done = sum(passes[:n]) + k
                        if done >= NO:
                            dve.wait_ge(one_hot_used, done - NO + 1)
                        row = C_ROW + n * LOOK_PASSES + k
                        dve.tensor_scalar(one_hot[done % NO], ids_row[n], cst[0:LOOK_ROWS, row:row + 1],
                                          None, ALU.is_equal).then_inc(one_hot_ready, 1)

                def block_lo_parts(m):
                    dve.wait_ge(block_hi, m + 1)
                    op = dve.tensor_tensor(xs[64:128, 2 * m, :], turned[0:64, :],
                                           xs[0:64, 2 * m, :].bitcast(F32), ALU.subtract)
                    if 2 * m + 1 < FIELDS - 1:
                        op = dve.tensor_tensor(xs[0:64, 2 * m + 1, :], turned[64:128, :],
                                               xs[64:128, 2 * m + 1, :].bitcast(F32), ALU.subtract)
                    op.then_inc(block_lo, 1)

                def chunk_lo_part(c):
                    dve.wait_ge(chunk_hi, c + 1)
                    dve.tensor_tensor(k_lo_buf(c), k_raw[:, c % NR, :],
                                      k_hi_buf(c).bitcast(F32), ALU.subtract).then_inc(chunk_lo, 1)

                def weighting(s):
                    dve.wait_ge(products_done, s + 1)
                    if s >= NW:
                        dve.wait_ge(sums_done, (s - NW) // 2 + 1)
                    dve.tensor_tensor(weighted[:, s % NW, :, :], product[:, s % NT, :, :],
                                      weighting_in1(s), ALU.mult).then_inc(weighted_dve, 1)

                dve.memset(dense_split[:, :].bitcast(F32), 0.0).then_inc(dense_zero, 1)
                dve.wait_ge(cst_look_in, 16)
                for n in range(LOOKS):
                    look(n)
                dve.wait_ge(dense_hi, 1)
                dve.tensor_tensor(dense_split[DENSE_LO_AT:DENSE_LO_AT + DENSE, :], dense_sb[:, :],
                                  dense_split[0:DENSE, :].bitcast(F32), ALU.subtract).then_inc(dense_lo, 1)
                for s in range(STEPS):
                    for c in k_lo_at.get(s, ()):
                        if c < POOL_CHUNK:
                            chunk_lo_part(c)
                    for m in x_lo_at.get(s, ()):
                        if m >= LOOKED:
                            block_lo_parts(m)
                    if not on_pool(s):
                        weighting(s)
                    if s == STEPS - SPLIT_AHEAD + 2:
                        dve.wait_ge(z_hi_done, 1)
                        dve.tensor_tensor(z_lo[:, 0:GROUPS - 1, :], z_kept, z_hi[:, 0:GROUPS - 1, :].bitcast(F32),
                                          ALU.subtract).then_inc(z_lo_done, 1)
                dve.wait_ge(z_hi_done, 2)
                dve.tensor_tensor(z_lo[:, GROUPS - 1, :], z_ps[:, :], z_hi[:, GROUPS - 1, :].bitcast(F32),
                                  ALU.subtract).then_inc(z_lo_done, 1)


def _constants():
    c = np.zeros((P, C_ALL), np.float32)
    c[:, C_EYE:C_EYE + P] = np.eye(P, dtype=np.float32)
    c[:, C_FOLD + 64:C_FOLD + P] = np.tile(np.eye(64, dtype=np.float32), (2, 1))
    for n in range(LOOKS):
        k = TABLE_ROWS[n] // LOOK_ROWS
        at = C_ROW + n * LOOK_PASSES
        c[:, at:at + k] = k * np.arange(P)[:, None] + np.arange(k)
    c[0:64, C_SEL + 30] = 1
    c[64:128, C_SEL + 31] = 1
    for t, (i, m) in enumerate(TILES):
        if i == 2 * m:
            g, row = z_row(t, 0)
            c[[m, DENSE_LO_AT + m], C_PLACE + g * P + row] = 1
    return c


def _layout(inputs):
    kernel_in = np.asarray(inputs["L0_rec_kernel"])
    w1_in = np.asarray(inputs["W_top1"])
    n_pairs = kernel_in.shape[1]
    pair_of = np.full(2 * len(TILES), -1)
    w1_row = np.zeros(GROUPS * P, int)
    for t, (i, m) in enumerate(TILES):
        for half in range(2):
            g, row = z_row(t, half)
            if 2 * m + half > i:
                pair_of[2 * t + half] = pair_index(i, 2 * m + half)
                w1_row[g * P + row] = pair_of[2 * t + half]
            else:
                w1_row[g * P + row] = n_pairs + m
    pairs = np.zeros((EMB, 2 * len(TILES), EMB), kernel_in.dtype)
    pairs[:, pair_of >= 0] = kernel_in[:, pair_of[pair_of >= 0]]
    arrays = {
        "dense_t": np.asarray(inputs["dense_ctx"]).T,
        "ids": np.asarray(inputs["ids"]),
        "ids_t": np.asarray(inputs["ids"]).T,
        "w1": w1_in[w1_row],
        "b1": np.asarray(inputs["b_top1"]).reshape(N1 // P, P).T,
        "w2": np.asarray(inputs["W_top2"]),
        "b2": np.asarray(inputs["b_top2"]).reshape(N2 // P, P).T,
        "w3": np.asarray(inputs["W_top3"]).reshape(N2 // P, P).T,
        "pairs": pairs.reshape(EMB, -1),
        "consts": _constants(),
    }
    for f in range(FIELDS):
        arrays[f"tbl_{f}"] = np.asarray(inputs[f"tbl_{f}"])
    return {name: np.ascontiguousarray(a) for name, a in arrays.items()}


def kernel(**inputs):
    import concourse.bacc as bacc
    from concourse.bass_utils import run_bass_kernel_spmd

    nc = bacc.Bacc("TRN2", target_bir_lowering=False, num_devices=1)
    arrays = _layout(inputs)
    dram = {
        name: nc.dram_tensor(name, a.shape, mybir.dt.from_np(a.dtype), kind="ExternalInput").ap()
        for name, a in arrays.items()
    }
    out = nc.dram_tensor("out", (BATCH, 1), F32, kind="ExternalOutput").ap()
    tower_kernel(
        nc, dram["dense_t"], dram["ids"], dram["ids_t"], [dram[f"tbl_{f}"] for f in range(FIELDS)], dram["w1"],
        dram["b1"], dram["w2"], dram["b2"], dram["w3"], dram["pairs"], dram["consts"],
        out.rearrange("(p t) o -> p (t o)", p=P),
    )
    r = run_bass_kernel_spmd(nc, [arrays], core_ids=[0])
    return r.results[0]["out"]
```

```python
from contextlib import ExitStack

import concourse.bass as bass
import numpy as np
from concourse import mybir

F32 = mybir.dt.float32
F32R = mybir.dt.float32r
I32 = mybir.dt.int32
U32 = mybir.dt.uint32
ALU = mybir.AluOpType
ACT = mybir.ActivationFunctionType

P = 128
BATCH, FIELDS, EMB, DENSE = 512, 32, 64, 16
N1, N2 = 512, 256
BT = BATCH // P
BLOCKS = FIELDS // 2
TILES = [(i, m) for m in range(BLOCKS) for i in range(2 * m + 1)]
STEPS = len(TILES) // 2
GROUP = 64
GROUPS = len(TILES) // GROUP
CHUNK = 8
CHUNKS = len(TILES) // CHUNK
CW = CHUNK * P
CS = CHUNK // 2

LOOK_BLOCKS = (0, 2)
LOOK_FIELDS = (31, 30, 29, 28)
LOOKS = [n for m in LOOK_BLOCKS for n in (2 * m, 2 * m + 1)]
HOLD_LOADS = 5
LOOK_ROWS = 125
LOOK_PASSES = 10
NO = 9
_gathered_fields = iter([f for f in reversed(range(FIELDS)) if f not in LOOK_FIELDS])
FIELD_OF = [LOOK_FIELDS[LOOKS.index(n)] if n in LOOKS else next(_gathered_fields) for n in range(FIELDS)]

NT = 3
NW = 8
NG = 4
NS = 2
NR = 3
NK = 5
GUESTS = 3
GUEST_AT = FIELDS - 2 - 4 * GUESTS

POOL_CHUNK = 25
POOL_STEP = 32
POOL_END = 118
POOL_EVERY = 4
TURN_AHEAD = (0, 1, 0, 2, 3, 4, 3, 5, 8, 6, 3, 5, 6, 5, 4, 6)
LO_AHEAD = (0, 0, 0, 1, 2, 2, 2, 3, 2, 3, 2, 2, 4, 3, 1, 4)
PE_LO = (4, 5, 7, 8)
HI_AT = (0, 1, 5, 5, 6, 7, 14, 18)
LO_AT = (0, 1, 5, 6, 6, 9, 13, 19)
K_AFTER = 9
GATHER_AHEAD = 15
SUMS_STEPS, SUMS_LAG = 4, 2

H1_AT = GROUPS
H2_AT = H1_AT + N1 // P
assert H2_AT + N2 // P < BLOCKS - 1

DENSE_LO_AT = 32

SEL = 62
FOLD = 64 + P
C_ROW = 0
C_FOLD = C_ROW + len(LOOKS) * LOOK_PASSES
C_EYE = C_FOLD + FOLD
C_SEL = C_EYE + P
C_PLACE = C_SEL + SEL
C_ALL = C_PLACE + GROUPS * P
TABLE_ROWS = (1250, 1000, 1000, 1250)


def pair_index(i, j):
    return i * (FIELDS - 1) - i * (i - 1) // 2 + (j - i - 1)


def z_row(tile, half):
    g, t = divmod(tile, GROUP)
    return g, 32 * (t % 4) + 2 * (t // 4) + half


def gathered_before(m):
    return sum(x not in LOOK_BLOCKS for x in range(m))


def dve_lo_blocks(m):
    return sum(x not in LOOK_BLOCKS + PE_LO for x in range(m))


def act_lo_blocks(m):
    return sum(x in PE_LO for x in range(m))


def block_steps(m):
    return m * m // 2


def on_pool(s):
    return POOL_STEP <= s < POOL_END and (s - POOL_STEP) % POOL_EVERY == 0


def pool_steps(s):
    return sum(on_pool(x) for x in range(s))


def tower_kernel(nc, dense_t, ids, ids_t, tables, w1, b1, w2, b2, w3, pairs, consts, out):
    turn_at = {}
    x_lo_at = {}
    for m in range(BLOCKS):
        turn_at.setdefault(block_steps(m) - TURN_AHEAD[m], []).append(m)
        x_lo_at.setdefault(block_steps(m) - LO_AHEAD[m], []).append(m)
    gather_at = {}
    for m in (m for m in range(BLOCKS) if m not in LOOK_BLOCKS):
        for k in range(2 * BT):
            at = block_steps(m) - m + m * k // (2 * BT) - GATHER_AHEAD
            gather_at.setdefault(max(0, at), []).append((m, k))
    k_lo_at = {}
    k_hi_at = {}
    for c in range(CHUNKS):
        k_hi_at.setdefault(HI_AT[c] if c < len(HI_AT) else CS * (c - NK) + K_AFTER - 2, []).append(c)
        k_lo_at.setdefault(LO_AT[c] if c < len(LO_AT) else CS * (c - NK) + K_AFTER, []).append(c)

    with ExitStack() as ctx:

        def sb(name, shape, dt=F32):
            return ctx.enter_context(nc.sbuf_tensor(name, shape, dt))

        def psum(name, shape):
            return ctx.enter_context(nc.psum_tensor(name, shape, F32))

        def sem(name):
            return ctx.enter_context(nc.semaphore(name))

        cst = sb("cst", [P, C_ALL])
        eye = cst[:, C_EYE:C_EYE + P]
        ids_sb = sb("ids_sb", [P, BT, FIELDS], I32)
        dense_sb = sb("dense_sb", [DENSE, BATCH])
        dense_split = sb("dense_split", [P, BATCH], F32R)
        place = sb("place", [P, GROUPS * P], F32R)
        gathered = sb("gathered", [P, NG, BT, 2 * EMB])
        xt = sb("xt", [P, BLOCKS, BATCH])
        xs = sb("xs", [P, FIELDS - 1, BATCH], F32R)
        guests = [
            [xs[:, n:n + 2, :].rearrange("p a b -> p (a b)") for n in (GUEST_AT + 4 * x, GUEST_AT + 4 * x + 2)]
            for x in reversed(range(GUESTS))
        ]
        passes = [rows // LOOK_ROWS for rows in TABLE_ROWS]
        table_raw = [
            xt[0:LOOK_ROWS, BLOCKS - 2 * (n + 1):BLOCKS - 2 * n, :].rearrange("p a b -> p (a b)")[:, 0:passes[n] * EMB]
            .rearrange("p (k e) -> p k e", e=EMB) for n in range(len(LOOKS))
        ]
        ids_row = [xt[0:LOOK_ROWS, BLOCKS - 2 * len(LOOKS) - 1 - n, :].bitcast(I32) for n in range(len(LOOKS))]
        table_split = [
            xs[0:LOOK_ROWS, n:n + 3, :].rearrange("p a b -> p (a b)")[:, 0:passes[x] * 2 * EMB]
            .rearrange("p (k h e) -> p k h e", h=2, e=EMB) for x, n in enumerate((8, 11, 8, 11))
        ]
        one_hot = [xs[0:LOOK_ROWS, n, :] for n in (*range(14, 14 + NO - 1), FIELDS - 2)]
        fold = sb("fold", [P, FOLD], F32R)
        minus = sb("minus", [P, P], F32R)
        block_hi_part = sb("block_hi_part", [P, BATCH], F32R)
        k_raw = sb("k_raw", [P, NR, CW])
        k_hi = sb("k_hi", [P, NK, CW], F32R)
        k_lo = sb("k_lo", [P, NK, CW], F32R)
        weighted = sb("weighted", [P, NW, 2, BATCH])
        staged = sb("staged", [P, NS, 2, BATCH])
        w1_sb = k_raw[:, 0:2, :].rearrange("p a (g n) -> p (a g) n", n=N1)
        w2_sb = k_raw[:, 2, :].rearrange("p (g n) -> p g n", n=N2)
        w3_sb = sb("w3_sb", [P, N2 // P])
        b1_sb = sb("b1_sb", [P, N1 // P])
        b2_sb = sb("b2_sb", [P, N2 // P])
        h1 = xt[:, H1_AT:H1_AT + N1 // P, :]
        h2 = xt[:, H2_AT:H2_AT + N2 // P, :]
        y_sb = xt[:, H2_AT + N2 // P, 0:BT]
        z = xt[:, 0:GROUPS, :]

        product = psum("product", [P, NT, 2, BATCH])
        z_ps = psum("z_ps", [P, BATCH])
        turned = psum("turned", [P, BATCH])

        ids_in = sem("ids_in")
        cst_look_in = sem("cst_look_in")
        cst_in = sem("cst_in")
        look_in = [sem(f"look_in{n}") for n in range(len(LOOKS))]
        fold_ready = sem("fold_ready")
        look_hi = sem("look_hi")
        look_lo = sem("look_lo")
        one_hot_ready = sem("one_hot_ready")
        one_hot_used = sem("one_hot_used")
        look_copied = sem("look_copied")
        dense_in = sem("dense_in")
        weights_in = sem("weights_in")
        raw_in = [sem(f"raw_in{r}") for r in range(NR)]
        block_in = [sem(f"block_in{g}") for g in range(NG)]
        block_turned = sem("block_turned")
        block_hi = sem("block_hi")
        block_lo = sem("block_lo")
        block_copied = sem("block_copied")
        lo_turned = sem("lo_turned")
        block_lo_act = sem("block_lo_act")
        chunk_hi = sem("chunk_hi")
        chunk_lo = sem("chunk_lo")
        chunk_lo_pool = sem("chunk_lo_pool")
        products_done = sem("products_done")
        staged_done = sem("staged_done")
        weighted_dve = sem("weighted_dve")
        weighted_pool = sem("weighted_pool")
        sums_done = sem("sums_done")
        dense_zero = sem("dense_zero")
        dense_hi = sem("dense_hi")
        dense_lo = sem("dense_lo")
        z_out = sem("z_out")
        h1_done = sem("h1_done")
        h1_ready = sem("h1_ready")
        h2_done = sem("h2_done")
        h2_ready = sem("h2_ready")
        y_done = sem("y_done")
        y_ready = sem("y_ready")
        y_out = sem("y_out")

        look_ps = [product[:, 0, 0, :], product[:, 0, 1, :], turned[:, :], turned[:, :]]
        fold_ps = {0: product[:, 1, 0, :], 2: turned[:, :]}
        at = [(STEPS - 3) % NT, (STEPS - 2) % NT, (STEPS - 1) % NT]
        h1_ps = [turned[:, :], product[:, at[0], 0, :], product[:, at[0], 1, :], product[:, at[1], 0, :]]
        h2_ps = [product[:, at[2], 0, :], product[:, at[2], 1, :]]
        y_ps = z_ps[:, 0:BT]

        def k_hi_buf(c):
            return guests[c - NK][0] if NK <= c < NK + GUESTS else k_hi[:, (c - GUESTS * (c >= NK)) % NK, :]

        def k_lo_buf(c):
            return guests[c - NK][1] if NK <= c < NK + GUESTS else k_lo[:, (c - GUESTS * (c >= NK)) % NK, :]

        def chunk_before(c):
            return c - NK if c - NK >= NK + GUESTS else c - NK - GUESTS

        def wait_block_read(eng, m):
            if m:
                eng.wait_ge(block_hi, m)
            if dve_lo_blocks(m):
                eng.wait_ge(block_lo, dve_lo_blocks(m))
            if act_lo_blocks(m):
                eng.wait_ge(block_lo_act, act_lo_blocks(m))

        def weighting_in1(s):
            m0, m1 = TILES[2 * s][1], TILES[2 * s + 1][1]
            if m0 == m1:
                return xt[:, m0:m0 + 1, :].to_broadcast([P, 2, BATCH])
            return xt[:, m0:m0 + 2, :]

        def wait_weighted(eng, steps):
            eng.wait_ge(weighted_dve, steps - pool_steps(steps))
            if pool_steps(steps):
                eng.wait_ge(weighted_pool, pool_steps(steps))

        def wait_product_free(eng, steps):
            eng.wait_ge(weighted_dve, steps - pool_steps(steps))
            if pool_steps(steps):
                eng.wait_ge(staged_done, pool_steps(steps))

        def wait_chunk_lo(eng, c):
            if c < POOL_CHUNK:
                eng.wait_ge(chunk_lo, c + 1)
            else:
                eng.wait_ge(chunk_lo_pool, c - POOL_CHUNK + 1)

        with nc.Block() as block:

            @block.sync
            def _(sp):
                sp.dma_start(ids_sb[:, :, :], ids.rearrange("(t p) f -> p t f", p=P)).then_inc(ids_in, 16)
                sp.dma_start(cst[:, 0:C_EYE], consts[:, 0:C_EYE]).then_inc(cst_look_in, 16)

                def load_look(n):
                    field = LOOK_FIELDS[n]
                    sp.dma_start(table_raw[n], tables[field].rearrange("(p k) e -> p k e", p=LOOK_ROWS))\
                        .then_inc(look_in[n], 16)
                    sp.dma_start(ids_row[n], ids_t[field:field + 1, :].to_broadcast([LOOK_ROWS, BATCH]))\
                        .then_inc(look_in[n], 16)

                load_look(0)
                load_look(1)
                for c in range(CHUNKS):
                    if c >= NR:
                        wait_chunk_lo(sp, c - NR)
                    if c == 1:
                        sp.wait_ge(one_hot_ready, HOLD_LOADS)
                    for half in range(2):
                        sp.dma_start(k_raw[64 * half:64 * half + 64, c % NR, :],
                                     pairs[:, c * CW:(c + 1) * CW]).then_inc(raw_in[c % NR], 16)
                    if c == 0:
                        sp.dma_start(cst[:, C_EYE:], consts[:, C_EYE:]).then_inc(cst_in, 16)
                        sp.dma_start(dense_sb[:, :], dense_t).then_inc(dense_in, 16)
                    if c == 1:
                        load_look(2)
                        load_look(3)
                wait_chunk_lo(sp, CHUNKS - 1)
                sp.dma_start(w1_sb, w1.rearrange("(g p) n -> p g n", p=P)).then_inc(weights_in, 16)
                sp.dma_start(w2_sb, w2.rearrange("(g p) n -> p g n", p=P)).then_inc(weights_in, 16)
                sp.dma_start(w3_sb[:, :], w3).then_inc(weights_in, 16)
                sp.dma_start(b1_sb[:, :], b1).then_inc(weights_in, 16)
                sp.dma_start(b2_sb[:, :], b2).then_inc(weights_in, 16)
                sp.wait_ge(y_ready, 1)
                sp.dma_start(out, y_sb).then_inc(y_out, 16)
                sp.wait_ge(y_out, 16)

            @block.gpsimd
            def _(pool):
                def gather(m, k):
                    n = gathered_before(m)
                    slot = n % NG
                    if n >= NG and k == 0:
                        pool.wait_ge(block_turned, m - NG + 1)
                    half, t = divmod(k, BT)
                    field = FIELD_OF[2 * m + half]
                    pool.indirect_dma_start(
                        gathered[:, slot, t, half * EMB:(half + 1) * EMB], None, tables[field],
                        bass.IndirectOffsetOnAxis(ap=ids_sb[:, t, field:field + 1].bitcast(U32), axis=0),
                    ).then_inc(block_in[slot], 16)

                def weighting(s):
                    pool.wait_ge(staged_done, pool_steps(s) + 1)
                    pool.wait_ge(sums_done, (s - NW) // 2 + 1)
                    pool.tensor_tensor(weighted[:, s % NW, :, :], staged[:, pool_steps(s) % NS, :, :],
                                       weighting_in1(s), ALU.mult).then_inc(weighted_pool, 1)

                pool.wait_ge(ids_in, 16)
                for s in range(STEPS):
                    for m, k in gather_at.get(s, ()):
                        gather(m, k)
                    for c in k_lo_at.get(s, ()):
                        if c >= POOL_CHUNK:
                            pool.wait_ge(chunk_hi, c + 1)
                            pool.tensor_tensor(k_lo_buf(c), k_raw[:, c % NR, :],
                                               k_hi_buf(c).bitcast(F32),
                                               ALU.subtract).then_inc(chunk_lo_pool, 1)
                    if on_pool(s):
                        weighting(s)

            @block.tensor
            def _(pe):
                def look_up(n):
                    if n >= 3:
                        pe.wait_ge(look_copied, n)
                    pe.wait_ge(look_hi, n + 1)
                    pe.wait_ge(look_lo, n + 1)
                    for k in range(passes[n]):
                        done = sum(passes[:n]) + k
                        pe.wait_ge(one_hot_ready, done + 1)
                        pe.matmul(look_ps[n], table_split[n][:, k, :, :], one_hot[done % NO],
                                  start=(k == 0), stop=(k == passes[n] - 1)).then_inc(one_hot_used, 1)

                def fold_block(m):
                    pe.wait_ge(fold_ready, 1)
                    pe.wait_ge(look_copied, 2 * LOOK_BLOCKS.index(m) + 2)
                    pe.matmul(fold_ps[m], fold[:, 64:64 + P], xs[:, 2 * m, :], start=True, stop=False)
                    pe.matmul(fold_ps[m], fold[:, 0:P], xs[:, 2 * m + 1, :], start=False, stop=True)\
                        .then_inc(block_turned, 1)

                def turn_block(m):
                    slot = gathered_before(m) % NG
                    pe.wait_ge(block_in[slot], 2 * BT * 16 * (gathered_before(m) // NG + 1))
                    if m > 1:
                        wait_block_read(pe, m)
                    for t in range(BT):
                        if m in PE_LO:
                            mm = pe.matmul(turned[:, t * P:(t + 1) * P], gathered[:, slot, t, :], eye,
                                           start=(t == 0), stop=False, skip_group_check=True)
                        else:
                            mm = pe.transpose(turned[:, t * P:(t + 1) * P], gathered[:, slot, t, :], eye)
                    mm.then_inc(block_turned, 1)

                def leave_lo(m):
                    pe.wait_ge(block_copied, act_lo_blocks(m) + 1)
                    pe.matmul(turned[:, :], minus[:, :], block_hi_part[:, :],
                              start=False, stop=True, skip_group_check=True).then_inc(lo_turned, 1)

                def products(s):
                    if s % CS == 0:
                        pe.wait_ge(chunk_hi, s // CS + 1)
                        wait_chunk_lo(pe, s // CS)
                    if s >= NT:
                        wait_product_free(pe, s - NT + 1)
                    for y in range(2):
                        t = 2 * s + y
                        i, m = TILES[t]
                        if i == 0:
                            wait_block_read(pe, m + 1)
                        col = slice((t % CHUNK) * P, (t % CHUNK + 1) * P)
                        c = t // CHUNK
                        pe.matmul(product[:, s % NT, y, :], k_hi_buf(c)[:, col], xs[:, i, :],
                                  start=True, stop=False)
                        mm = pe.matmul(product[:, s % NT, y, :], k_lo_buf(c)[:, col], xs[:, i, :],
                                       start=False, stop=True)
                    mm.then_inc(products_done, 1)

                def sums(q):
                    g, at = divmod(q, GROUP // 4)
                    if at == 0:
                        if g >= 1:
                            pe.wait_ge(z_out, g)
                        else:
                            pe.wait_ge(dense_lo, 1)
                        pe.matmul(z_ps[:, :], place[:, g * P:(g + 1) * P],
                                  dense_split[:, :], start=True, stop=False, skip_group_check=True)
                    wait_weighted(pe, 2 * q + 2)
                    for c in range(4):
                        mm = pe.matmul(z_ps[32 * c:32 * c + 32, :],
                                       cst[:, C_SEL + 30 - 2 * at:C_SEL + 62 - 2 * at],
                                       weighted[:, (2 * q + c // 2) % NW, c % 2, :],
                                       start=False, stop=(at == GROUP // 4 - 1), skip_group_check=True)
                    mm.then_inc(sums_done, 1)

                look_up(0)
                look_up(1)
                pe.wait_ge(cst_in, 16)
                turn_block(1)
                fold_block(0)
                wait_block_read(pe, 2)
                for s in range(STEPS):
                    for m in turn_at.get(s, ()):
                        if m not in LOOK_BLOCKS + (1,):
                            turn_block(m)
                        elif m > 1:
                            wait_block_read(pe, m)
                            look_up(2)
                            look_up(3)
                            fold_block(m)
                    for m in x_lo_at.get(s, ()):
                        if m in PE_LO:
                            leave_lo(m)
                    products(s)
                    done = s + 1 - SUMS_LAG
                    if done > 0 and done % SUMS_STEPS == 0:
                        for q in range((done - SUMS_STEPS) // 2, done // 2):
                            sums(q)

                def layer_1(n, groups):
                    for g in groups:
                        mm = pe.matmul(h1_ps[n], w1_sb[:, g, n * P:(n + 1) * P], z[:, g, :],
                                       start=(g == 0), stop=(g == GROUPS - 1))
                    return mm

                pe.wait_ge(weights_in, 5 * 16)
                wait_block_read(pe, BLOCKS)
                layer_1(0, range(GROUPS - 1))
                wait_product_free(pe, STEPS - 2)
                layer_1(1, range(GROUPS - 1))
                layer_1(2, range(GROUPS - 1))
                for q in range((STEPS - SUMS_STEPS) // 2, STEPS // 2):
                    sums(q)
                wait_product_free(pe, STEPS - 1)
                layer_1(3, range(GROUPS - 1))
                pe.wait_ge(z_out, GROUPS)
                for n in range(N1 // P):
                    layer_1(n, [GROUPS - 1]).then_inc(h1_done, 1)

                wait_product_free(pe, STEPS)
                for g in range(N1 // P):
                    pe.wait_ge(h1_ready, g + 1)
                    for n in range(N2 // P):
                        mm = pe.matmul(h2_ps[n], w2_sb[:, g, n * P:(n + 1) * P], h1[:, g, :],
                                       start=(g == 0), stop=(g == N1 // P - 1))
                        if g == N1 // P - 1:
                            mm.then_inc(h2_done, 1)
                for g in range(N2 // P):
                    pe.wait_ge(h2_ready, g + 1)
                    for t in range(BT):
                        mm = pe.matmul(y_ps[:, t:t + 1], h2[:, g, t::BT], w3_sb[:, g:g + 1],
                                       start=(g == 0 and t == 0), stop=(g == N2 // P - 1), skip_group_check=True)
                mm.then_inc(y_done, 1)

            @block.scalar
            def _(act):
                def look_hi_part(n):
                    act.wait_ge(look_in[n], 32)
                    if n >= 2:
                        act.wait_ge(one_hot_used, sum(passes[:n - 1]))
                    act.activation(table_split[n][:, :, 0, :], table_raw[n], ACT.Copy).then_inc(look_hi, 1)

                def copy_looked_up(n):
                    act.wait_ge(one_hot_used, sum(passes[:n + 1]))
                    act.activation(xs[:, LOOKS[n], :], look_ps[n], ACT.Copy).then_inc(look_copied, 1)

                def copy_folded(m):
                    act.wait_ge(block_turned, max(2, m + 1))
                    act.activation(xt[:, m, :], fold_ps[m], ACT.Copy).then_inc(block_hi, 1)

                def block_hi_parts(m):
                    act.wait_ge(block_turned, m + 1 if m > 1 else 1)
                    if m == GUEST_AT // 2:
                        act.wait_ge(products_done, CS * (NK + GUESTS))
                    if m in PE_LO:
                        act.activation(block_hi_part[:, :], turned[:, :], ACT.Copy)
                        act.activation(xt[:, m, :], turned[:, :], ACT.Copy).then_inc(block_copied, 1)
                        act.wait_ge(block_copied, act_lo_blocks(m) + 1)
                        act.activation(xs[0:64, 2 * m, :], block_hi_part[0:64, :].bitcast(F32), ACT.Copy)
                        act.activation(xs[64:128, 2 * m + 1, :], block_hi_part[64:128, :].bitcast(F32),
                                       ACT.Copy).then_inc(block_hi, 1)
                        return
                    act.activation(xs[0:64, 2 * m, :], turned[0:64, :], ACT.Copy)
                    if 2 * m + 1 < FIELDS - 1:
                        act.activation(xs[64:128, 2 * m + 1, :], turned[64:128, :], ACT.Copy)
                    act.activation(xt[:, m, :], turned[:, :], ACT.Copy).then_inc(block_hi, 1)

                def block_lo_act_parts(m):
                    act.wait_ge(lo_turned, act_lo_blocks(m) + 1)
                    act.activation(xs[64:128, 2 * m, :], turned[0:64, :], ACT.Copy)
                    act.activation(xs[0:64, 2 * m + 1, :], turned[64:128, :], ACT.Copy).then_inc(block_lo_act, 1)

                def chunk_hi_part(c):
                    if NK <= c < NK + GUESTS:
                        act.wait_ge(one_hot_used, sum(passes))
                    act.wait_ge(raw_in[c % NR], 32 * (c // NR + 1))
                    if c >= NK + GUESTS:
                        act.wait_ge(products_done, CS * (chunk_before(c) + 1))
                    act.activation(k_hi_buf(c), k_raw[:, c % NR, :], ACT.Copy).then_inc(chunk_hi, 1)

                def keep_z(g):
                    act.wait_ge(sums_done, (g + 1) * GROUP // 4)
                    act.activation(z[:, g, :], z_ps[:, :], ACT.Copy).then_inc(z_out, 1)

                def stage(s):
                    act.wait_ge(products_done, s + 1)
                    n = pool_steps(s)
                    if n >= NS:
                        act.wait_ge(weighted_pool, n - NS + 1)
                    act.activation(staged[:, n % NS, :, :], product[:, s % NT, :, :],
                                   ACT.Copy).then_inc(staged_done, 1)

                act.wait_ge(cst_look_in, 16)
                act.activation(fold[:, :], cst[:, C_FOLD:C_FOLD + FOLD], ACT.Copy).then_inc(fold_ready, 1)
                look_hi_part(0)
                look_hi_part(1)
                act.wait_ge(dense_in, 16)
                act.wait_ge(cst_in, 16)
                act.wait_ge(dense_zero, 1)
                act.activation(dense_split[0:DENSE, :], dense_sb[:, :], ACT.Copy)
                act.activation(minus[:, :], eye, ACT.Copy, scale=-1.0)
                act.activation(place[:, :], cst[:, C_PLACE:C_PLACE + GROUPS * P], ACT.Copy).then_inc(dense_hi, 1)
                for s in range(STEPS):
                    for c in k_hi_at.get(s, ()):
                        chunk_hi_part(c)
                    for m in turn_at.get(s, ()):
                        if m == 0:
                            copy_looked_up(0)
                            copy_looked_up(1)
                            block_hi_parts(1)
                            copy_folded(0)
                            look_hi_part(2)
                            look_hi_part(3)
                        elif m == 2:
                            copy_looked_up(2)
                            copy_looked_up(3)
                            copy_folded(2)
                        elif m > 2:
                            block_hi_parts(m)
                    for m in x_lo_at.get(s, ()):
                        if m in PE_LO:
                            block_lo_act_parts(m)
                    if s % (GROUP // 2) == SUMS_LAG and s > SUMS_LAG:
                        keep_z(s // (GROUP // 2) - 1)
                    if on_pool(s):
                        stage(s)
                keep_z(GROUPS - 1)
                act.wait_ge(weights_in, 5 * 16)
                for n in range(N1 // P):
                    act.wait_ge(h1_done, n + 1)
                    act.activation(h1[:, n, :], h1_ps[n], ACT.Relu,
                                   bias=b1_sb[:, n:n + 1]).then_inc(h1_ready, 1)
                for n in range(N2 // P):
                    act.wait_ge(h2_done, n + 1)
                    act.activation(h2[:, n, :], h2_ps[n], ACT.Relu,
                                   bias=b2_sb[:, n:n + 1]).then_inc(h2_ready, 1)
                act.wait_ge(y_done, 1)
                act.activation(y_sb, y_ps, ACT.Copy).then_inc(y_ready, 1)

            @block.vector
            def _(dve):
                def look(n):
                    dve.wait_ge(look_hi, n + 1)
                    dve.tensor_tensor(table_split[n][:, :, 1, :], table_raw[n],
                                      table_split[n][:, :, 0, :].bitcast(F32), ALU.subtract).then_inc(look_lo, 1)
                    for k in range(passes[n]):
                        done = sum(passes[:n]) + k
                        if done >= NO:
                            dve.wait_ge(one_hot_used, done - NO + 1)
                        row = C_ROW + n * LOOK_PASSES + k
                        dve.tensor_scalar(one_hot[done % NO], ids_row[n], cst[0:LOOK_ROWS, row:row + 1],
                                          None, ALU.is_equal).then_inc(one_hot_ready, 1)

                def block_lo_parts(m):
                    dve.wait_ge(block_hi, m + 1 if m > 1 else 1)
                    op = dve.tensor_tensor(xs[64:128, 2 * m, :], turned[0:64, :],
                                           xs[0:64, 2 * m, :].bitcast(F32), ALU.subtract)
                    if 2 * m + 1 < FIELDS - 1:
                        op = dve.tensor_tensor(xs[0:64, 2 * m + 1, :], turned[64:128, :],
                                               xs[64:128, 2 * m + 1, :].bitcast(F32), ALU.subtract)
                    op.then_inc(block_lo, 1)

                def chunk_lo_part(c):
                    dve.wait_ge(chunk_hi, c + 1)
                    dve.tensor_tensor(k_lo_buf(c), k_raw[:, c % NR, :],
                                      k_hi_buf(c).bitcast(F32), ALU.subtract).then_inc(chunk_lo, 1)

                def weighting(s):
                    dve.wait_ge(products_done, s + 1)
                    if s >= NW:
                        dve.wait_ge(sums_done, (s - NW) // 2 + 1)
                    dve.tensor_tensor(weighted[:, s % NW, :, :], product[:, s % NT, :, :],
                                      weighting_in1(s), ALU.mult).then_inc(weighted_dve, 1)

                dve.memset(dense_split[:, :].bitcast(F32), 0.0).then_inc(dense_zero, 1)
                dve.wait_ge(cst_look_in, 16)
                look(0)
                look(1)
                dve.wait_ge(dense_hi, 1)
                dve.tensor_tensor(dense_split[DENSE_LO_AT:DENSE_LO_AT + DENSE, :], dense_sb[:, :],
                                  dense_split[0:DENSE, :].bitcast(F32), ALU.subtract).then_inc(dense_lo, 1)
                for s in range(STEPS):
                    for c in k_lo_at.get(s, ()):
                        if c < POOL_CHUNK:
                            chunk_lo_part(c)
                    for m in x_lo_at.get(s, ()):
                        if m not in LOOK_BLOCKS + PE_LO:
                            block_lo_parts(m)
                    if s == 0:
                        look(2)
                        look(3)
                    if not on_pool(s):
                        weighting(s)


def _constants():
    c = np.zeros((P, C_ALL), np.float32)
    c[:, C_EYE:C_EYE + P] = np.eye(P, dtype=np.float32)
    c[:, C_FOLD + 64:C_FOLD + P] = np.tile(np.eye(64, dtype=np.float32), (2, 1))
    for n in range(len(LOOKS)):
        k = TABLE_ROWS[n] // LOOK_ROWS
        at = C_ROW + n * LOOK_PASSES
        c[:, at:at + k] = k * np.arange(P)[:, None] + np.arange(k)
    c[0:64, C_SEL + 30] = 1
    c[64:128, C_SEL + 31] = 1
    for t, (i, m) in enumerate(TILES):
        if i == 2 * m:
            g, row = z_row(t, 0)
            c[[m, DENSE_LO_AT + m], C_PLACE + g * P + row] = 1
    return c


def _layout(inputs):
    kernel_in = np.asarray(inputs["L0_rec_kernel"])
    w1_in = np.asarray(inputs["W_top1"])
    n_pairs = kernel_in.shape[1]
    pairs = np.zeros((EMB, 2 * len(TILES), EMB), kernel_in.dtype)
    w1_row = np.zeros(GROUPS * P, int)
    for t, (i, m) in enumerate(TILES):
        for half in range(2):
            g, row = z_row(t, half)
            if 2 * m + half > i:
                contracted, other = FIELD_OF[i], FIELD_OF[2 * m + half]
                pair = pair_index(min(contracted, other), max(contracted, other))
                matrix = kernel_in[:, pair, :]
                pairs[:, 2 * t + half, :] = matrix if contracted > other else matrix.T
                w1_row[g * P + row] = pair
            else:
                w1_row[g * P + row] = n_pairs + m
    arrays = {
        "dense_t": np.asarray(inputs["dense_ctx"]).T,
        "ids": np.asarray(inputs["ids"]),
        "ids_t": np.asarray(inputs["ids"]).T,
        "w1": w1_in[w1_row],
        "b1": np.asarray(inputs["b_top1"]).reshape(N1 // P, P).T,
        "w2": np.asarray(inputs["W_top2"]),
        "b2": np.asarray(inputs["b_top2"]).reshape(N2 // P, P).T,
        "w3": np.asarray(inputs["W_top3"]).reshape(N2 // P, P).T,
        "pairs": pairs.reshape(EMB, -1),
        "consts": _constants(),
    }
    for f in range(FIELDS):
        arrays[f"tbl_{f}"] = np.asarray(inputs[f"tbl_{f}"])
    return {name: np.ascontiguousarray(a) for name, a in arrays.items()}


def kernel(**inputs):
    import concourse.bacc as bacc
    from concourse.bass_utils import run_bass_kernel_spmd

    nc = bacc.Bacc("TRN2", target_bir_lowering=False, num_devices=1)
    arrays = _layout(inputs)
    dram = {
        name: nc.dram_tensor(name, a.shape, mybir.dt.from_np(a.dtype), kind="ExternalInput").ap()
        for name, a in arrays.items()
    }
    out = nc.dram_tensor("out", (BATCH, 1), F32, kind="ExternalOutput").ap()
    tower_kernel(
        nc, dram["dense_t"], dram["ids"], dram["ids_t"], [dram[f"tbl_{f}"] for f in range(FIELDS)], dram["w1"],
        dram["b1"], dram["w2"], dram["b2"], dram["w3"], dram["pairs"], dram["consts"],
        out.rearrange("(p t) o -> p (t o)", p=P),
    )
    r = run_bass_kernel_spmd(nc, [arrays], core_ids=[0])
    return r.results[0]["out"]
```
